# Optimizing a Trainium2 kernel written in Bass

```python
import numpy as np
import jax
import jax.numpy as jnp

def _softmax(x, axis=-1):
    return jax.nn.softmax(x, axis=axis)

def _gelu(x):
    return jax.nn.gelu(x, approximate=True)

def _silu(x):
    return jax.nn.silu(x)

def _sigmoid(x):
    return jax.nn.sigmoid(x)

def _layernorm(x, axis=-1, eps=1e-05):
    m = jnp.mean(x, axis=axis, keepdims=True)
    v = jnp.var(x, axis=axis, keepdims=True)
    return (x - m) / jnp.sqrt(v + eps)

def _scatter_add(tgt, idx, src, axis=0):
    return tgt.at[idx].add(src)

def _segment_sum(src, seg, n):
    return jax.ops.segment_sum(src, seg, n)
kernel_name = 'mk_prb_d1_jaxref_r8_3d02a6'

def setup_inputs(seed: int=0):
    np.random.seed(seed)
    _w = jnp.asarray

    def _L0_attn_setup():
        import jax, jax.numpy as jnp
        import numpy as np
        D_MODEL = 128
        D_STATE = 16
        EXPAND = 2
        D_INNER = EXPAND * D_MODEL
        BATCH = 8
        SEQ = 256

        def _linear_init(key, fan_in, shape):
            bound = 1.0 / np.sqrt(fan_in)
            return jax.random.uniform(key, shape, jnp.float32, -bound, bound)

        def _silu(v):
            return v * jax.nn.sigmoid(v)
        key = jax.random.key(seed)
        ks = jax.random.split(key, 9)
        x = jax.random.normal(ks[0], (BATCH, SEQ, D_MODEL), jnp.float32)
        W_in = _linear_init(ks[1], D_MODEL, (D_MODEL, 2 * D_INNER))
        b_in = _linear_init(ks[2], D_MODEL, (2 * D_INNER,))
        W_x = _linear_init(ks[3], D_INNER, (D_INNER, 2 * D_STATE))
        b_x = _linear_init(ks[4], D_INNER, (2 * D_STATE,))
        W_dt = _linear_init(ks[5], D_INNER, (D_INNER, D_INNER))
        b_dt = _linear_init(ks[6], D_INNER, (D_INNER,))
        W_out = _linear_init(ks[7], D_INNER, (D_INNER, D_MODEL))
        b_out = _linear_init(ks[8], D_INNER, (D_MODEL,))
        A = jnp.tile(jnp.arange(1, D_STATE + 1, dtype=jnp.float32), (D_INNER, 1))
        A_log = jnp.log(A)
        D_param = jnp.ones((D_INNER,), jnp.float32)
        return dict(x=x, W_in=W_in, b_in=b_in, W_x=W_x, b_x=b_x, W_dt=W_dt, b_dt=b_dt, W_out=W_out, b_out=b_out, A_log=A_log, D_param=D_param)
    _L0_attn_in = _L0_attn_setup()

    def _L0_ffn_setup():
        import jax, jax.numpy as jnp
        import numpy as np
        BEST_K = 2

        def _expert(xf, w1, w3, w2):
            return jax.nn.silu(xf @ w1) * (xf @ w3) @ w2
        key = jax.random.key(seed)
        ks = jax.random.split(key, 9)
        E, S_sh, D, H = (8, 2, 128, 64)
        B, S = (2, 256)
        w = lambda k, shape: jax.random.normal(k, shape, dtype=jnp.float32) * 0.02
        return {'x': jax.random.normal(ks[0], (B, S, D), dtype=jnp.float32), 'router_w': w(ks[1], (D, E)), 'router_b': jnp.zeros((E,), dtype=jnp.float32), 'routed_w1': w(ks[2], (E, D, H)), 'routed_w3': w(ks[3], (E, D, H)), 'routed_w2': w(ks[4], (E, H, D)), 'shared_w1': w(ks[5], (S_sh, D, H)), 'shared_w3': w(ks[6], (S_sh, D, H)), 'shared_w2': w(ks[7], (S_sh, H, D))}
    _L0_ffn_in = _L0_ffn_setup()
    _d = {'L0_attn_x': _L0_attn_in['x'], 'L0_attn_W_in': _L0_attn_in['W_in'], 'L0_attn_b_in': _L0_attn_in['b_in'], 'L0_attn_W_x': _L0_attn_in['W_x'], 'L0_attn_b_x': _L0_attn_in['b_x'], 'L0_attn_W_dt': _L0_attn_in['W_dt'], 'L0_attn_b_dt': _L0_attn_in['b_dt'], 'L0_attn_W_out': _L0_attn_in['W_out'], 'L0_attn_b_out': _L0_attn_in['b_out'], 'L0_attn_A_log': _L0_attn_in['A_log'], 'L0_attn_D_param': _L0_attn_in['D_param'], 'L0_ffn_router_w': _L0_ffn_in['router_w'], 'L0_ffn_router_b': _L0_ffn_in['router_b'], 'L0_ffn_routed_w1': _L0_ffn_in['routed_w1'], 'L0_ffn_routed_w3': _L0_ffn_in['routed_w3'], 'L0_ffn_routed_w2': _L0_ffn_in['routed_w2'], 'L0_ffn_shared_w1': _L0_ffn_in['shared_w1'], 'L0_ffn_shared_w3': _L0_ffn_in['shared_w3'], 'L0_ffn_shared_w2': _L0_ffn_in['shared_w2']}
    _x0 = _d['L0_attn_x']
    _d['L0_attn_x'] = jax.random.normal(jax.random.fold_in(jax.random.key(seed), 1), (2, 2048, 128), dtype=_x0.dtype)
    del _x0
    return _d

def reference(L0_attn_x, L0_attn_W_in, L0_attn_b_in, L0_attn_W_x, L0_attn_b_x, L0_attn_W_dt, L0_attn_b_dt, L0_attn_W_out, L0_attn_b_out, L0_attn_A_log, L0_attn_D_param, L0_ffn_router_w, L0_ffn_router_b, L0_ffn_routed_w1, L0_ffn_routed_w3, L0_ffn_routed_w2, L0_ffn_shared_w1, L0_ffn_shared_w3, L0_ffn_shared_w2):

    def _L0_attn_ref(x, W_in, b_in, W_x, b_x, W_dt, b_dt, W_out, b_out, A_log, D_param):
        import jax, jax.numpy as jnp
        import numpy as np
        D_MODEL = 128
        D_STATE = 16
        EXPAND = 2
        D_INNER = EXPAND * D_MODEL
        BATCH = 8
        SEQ = 256

        def _linear_init(key, fan_in, shape):
            bound = 1.0 / np.sqrt(fan_in)
            return jax.random.uniform(key, shape, jnp.float32, -bound, bound)

        def _silu(v):
            return v * jax.nn.sigmoid(v)
        xz = x @ W_in + b_in
        x_proj, z = jnp.split(xz, 2, axis=-1)
        u = _silu(x_proj)
        A = -jnp.exp(A_log)
        x_dbl = u @ W_x + b_x
        Bm, Cm = jnp.split(x_dbl, 2, axis=-1)
        dt = jax.nn.softplus(u @ W_dt + b_dt)
        uT = jnp.swapaxes(u, 0, 1)
        dtT = jnp.swapaxes(dt, 0, 1)
        BT = jnp.swapaxes(Bm, 0, 1)
        CT = jnp.swapaxes(Cm, 0, 1)

        def step(h, inp):
            u_t, dt_t, B_t, C_t = inp
            dA = jnp.exp(dt_t[..., None] * A)
            h = h * dA + (dt_t * u_t)[..., None] * B_t[:, None, :]
            y_t = jnp.einsum('bds,bs->bd', h, C_t) + D_param * u_t
            return (h, y_t)
        h0 = jnp.zeros((x.shape[0], D_INNER, D_STATE), x.dtype)
        _, yT = jax.lax.scan(step, h0, (uT, dtT, BT, CT))
        y = jnp.swapaxes(yT, 0, 1)
        y = y * _silu(z)
        return y @ W_out + b_out

    def _L0_ffn_ref(x, router_w, router_b, routed_w1, routed_w3, routed_w2, shared_w1, shared_w3, shared_w2):
        import jax, jax.numpy as jnp
        import numpy as np
        BEST_K = 2

        def _expert(xf, w1, w3, w2):
            return jax.nn.silu(xf @ w1) * (xf @ w3) @ w2
        B, S, D = x.shape
        T = B * S
        xf = x.reshape(T, D)
        logits = xf @ router_w + router_b
        topk_vals, topk_idx = jax.lax.top_k(logits, BEST_K)
        sparse = jnp.full_like(logits, -jnp.inf)
        sparse = sparse.at[jnp.arange(T)[:, None], topk_idx].set(topk_vals)
        gates = jax.nn.softmax(sparse, axis=-1)
        routed = jax.vmap(_expert, in_axes=(None, 0, 0, 0))(xf, routed_w1, routed_w3, routed_w2)
        routed_out = jnp.einsum('etd,te->td', routed, gates)
        shared_out = jax.vmap(_expert, in_axes=(None, 0, 0, 0))(xf, shared_w1, shared_w3, shared_w2).sum(axis=0)
        return (routed_out + shared_out).reshape(B, S, D)
    x = L0_attn_x
    xn = _layernorm(x, axis=-1)
    x = x + _L0_attn_ref(xn, L0_attn_W_in, L0_attn_b_in, L0_attn_W_x, L0_attn_b_x, L0_attn_W_dt, L0_attn_b_dt, L0_attn_W_out, L0_attn_b_out, L0_attn_A_log, L0_attn_D_param) + _L0_ffn_ref(xn, L0_ffn_router_w, L0_ffn_router_b, L0_ffn_routed_w1, L0_ffn_routed_w3, L0_ffn_routed_w2, L0_ffn_shared_w1, L0_ffn_shared_w3, L0_ffn_shared_w2)
    return x

_drawn_inputs = setup_inputs


def setup_inputs(seed=0):
    import zlib

    import numpy as np

    out = dict(_drawn_inputs(seed))
    spreads = {'L0_attn_D_param': (1.0, 0.6), 'L0_ffn_router_b': (0.0, 0.8)}
    factors = {'L0_attn_b_in': 7.048,
     'L0_attn_W_x': 8.0,
     'L0_attn_b_x': 8.0,
     'L0_attn_W_dt': 8.0,
     'L0_attn_b_dt': 8.0,
     'L0_attn_A_log': 8.0,
     'L0_ffn_router_w': 8.0,
     'L0_ffn_routed_w1': 8.0,
     'L0_ffn_routed_w3': 8.0,
     'L0_ffn_routed_w2': 8.0,
     'L0_ffn_shared_w1': 8.0,
     'L0_ffn_shared_w3': 8.0,
     'L0_ffn_shared_w2': 8.0,
     'L0_attn_b_out': 7.206}
    for name, (base, spread) in spreads.items():
        noise = np.random.default_rng([zlib.crc32(name.encode()), seed]).standard_normal(out[name].shape)
        drawn = base * np.exp(spread * noise) if base else spread * noise
        out[name] = jnp.asarray(drawn.astype(out[name].dtype))
    for name, factor in factors.items():
        out[name] = (out[name] * factor).astype(out[name].dtype)
    return out
```

```python
import concourse.bass as bass
from concourse import mybir
from contextlib import ExitStack

F32 = mybir.dt.float32
BF16 = mybir.dt.bfloat16
U32 = mybir.dt.uint32
ALU = mybir.AluOpType
ACT = mybir.ActivationFunctionType
EXP_LN_SET = "natural_log_exp_and_others"

P = 128
BATCH, SEQ, D = 2, 2048, 128
INNER, STATES = 256, 16
KD = INNER // P
EXPERTS, SHARED, H = 8, 2, 64
EPT = P // H
RT = EXPERTS // EPT
ET = (EXPERTS + SHARED) // EPT
CHUNK = 512
NT = CHUNK // P
CHUNKS = BATCH * SEQ // CHUNK
CPB = SEQ // CHUNK
PARTS = 3
BC = 2 * STATES
SPREAD = PARTS * (BC + EXPERTS)
EPS = 1e-5
BIG = 3.4028234e38

POOL_B = [s for s in range(STATES) if s % 2 == 1]
DVE_B = [s for s in range(STATES) if s not in POOL_B]
C_RING, Y_RING, BX_RING, H_RING, DECAY_RING = 4, 4, 2, 8, 4
assert len(POOL_B) % BX_RING == 0 and len(DVE_B) % BX_RING == 0
N_FIRST, N_WEIGHTS, N_SMALL = 5, 6, 10 + 2 * PARTS
ACT_STEPS, DVE_STEPS = 2 * 4, 2 * 6

SLOT = {"T0": 2, "R0": 3, "Z0": 3, "Z1": 4, "Z2": 4, "Z3": 5, "A0": 5, "O0": 6, "A1": 6, "X0": 7, "A2": 7,
        "D0": 8, "A3": 8, "D1": 9, "A4": 9, "O1": 9, "O2": 10, "O3": 10, "M0": 11, "G0": 12, "M1": 12,
        "G1": 13, "M2": 13, "G2": 14, "M3": 14, "G3": 15, "M4": 15}
JOBS = list(SLOT)
JOB_BANKS, B_BANKS = 3, 2
while len(JOBS) % JOB_BANKS:
    JOBS.append("--")
BANK = {job: i % JOB_BANKS for i, job in enumerate(JOBS)}
SPREAD_B, COPY_B, SPREAD_C, COPY_C, DECAY, BX, TIMES_C, SUM = 3, 3, 2, 2, 2, 2, -1, -2
STATS, RSTD, NORM, SKIP, FINISH_Y, TOP2, RATIO, GATES = 0, 0, 1, 2, 3, 4, 5, 6
SILU_XZ, REST_1, PART_2, REST_2, DTU, SILU_UP, RESIDUAL = 6, 9, 10, 11, 12, 10, 4


class Chunk:

    def __init__(self, k, turn=None):
        self.k, self.turn, self.parity = k, turn, k % 2

    def __add__(self, d):
        return Chunk(self.k + d, self.turn)

    def count(self, per, more):
        v = per * self.k + more
        return v if self.turn is None else self.turn * (2 * per) + v

    @property
    def index(self):
        return self.count(1, 0)

    def since(self, k):
        return self.turn is not None or self.k >= k

    @property
    def real(self):
        return self.turn is not None or 0 <= self.k < CHUNKS


class Steps:

    def __init__(self):
        self.n, self.turn, self.per = 0, None, 0

    def next(self):
        self.n += 1
        return self.n if self.turn is None else self.turn * self.per + self.n

    def enter(self, turn, per):
        self.turn, self.per, self.base = turn, per, self.n

    def leave(self, turns):
        assert self.n - self.base == self.per, (self.n - self.base, self.per)
        self.n, self.turn = self.base + turns * self.per, None


def job_before(n, job):
    i = JOBS.index(job) - JOB_BANKS
    while True:
        m = n if i >= 0 else n + -1
        before = JOBS[i % len(JOBS)]
        if before == "--" or not job_lives(m, before):
            i -= JOB_BANKS
            if m.turn is None and m.k < 0:
                return None
            if i < -len(JOBS):
                return None
            continue
        return m, before


def job_lives(n, job):
    return n.turn is not None or (0 <= n.k - 2 < CHUNKS if job[0] == "O" else n.real)


def at_state(c, slot, ahead):
    return c + (slot + ahead) // STATES, (slot + ahead) % STATES


def mixed_layer_program(nc, x, W_in, b_in, W_x, b_x, W_dt, b_dt, W_out, b_out, A_log, D_param,
                        router_w, router_b, routed_w1, routed_w3, routed_w2,
                        shared_w1, shared_w3, shared_w2, ident_c, rows_c, part_mask_c, iota_c, keep_c, out):
    x_v = x.rearrange("b s d -> (b s) d").rearrange("(c n p) d -> c p n d", n=NT, p=P)
    out_v = out.rearrange("b s d -> (b s) d").rearrange("(c n p) d -> c p n d", n=NT, p=P)
    ctx = ExitStack()
    with ctx:
        def sb(name, shape, dt=F32):
            return ctx.enter_context(nc.sbuf_tensor(name, shape, dt))

        def pb(name, shape):
            return ctx.enter_context(nc.psum_tensor(name, shape, F32))

        def sem(name):
            return ctx.enter_context(nc.semaphore(name))

        w_in = sb("w_in", [P, 2 * INNER])
        w_x3 = sb("w_x3", [P, KD, PARTS * BC])
        w_dt = sb("w_dt", [P, KD, INNER])
        w_out = sb("w_out", [P, KD, D])
        w_r = sb("w_r", [P, EXPERTS])
        w1 = sb("w1", [P, EXPERTS + SHARED, H])
        w3 = sb("w3", [P, EXPERTS + SHARED, H])
        w2 = sb("w2", [P, ET, D])
        bias_in = sb("bias_in", [P, 2 * KD])
        bias_x3 = sb("bias_x3", [SPREAD, 1])
        bias_dt = sb("bias_dt", [P, KD])
        bias_out = sb("bias_out", [P, D])
        bias_r = sb("bias_r", [P, EXPERTS])
        d_par = sb("d_par", [P, KD])
        a_log = sb("a_log", [P, KD, STATES])
        a_neg = sb("a_neg", [P, KD, STATES])
        ident = sb("ident", [P, P])
        selector = sb("selector", [SPREAD, BC + RT, P], BF16)
        rows = sb("rows", [SPREAD, BC + EXPERTS])
        part_mask = sb("part_mask", [SPREAD, 2])
        iota = sb("iota", [P, EXPERTS])
        keep = sb("keep", [P, 2, CHUNKS])
        minus_half = sb("minus_half", [P, NT])
        eps = sb("eps", [P, NT])
        seat = sb("seat", [P, 1])

        x_t = sb("x_t", [P, 2, NT, D])
        x_res = sb("x_res", [P, NT, D])
        stats = sb("stats", [P, NT, 6])
        mean_var = sb("mean_var", [P, NT, 2])
        var_eps = sb("var_eps", [P, NT])
        rstd = sb("rstd", [P, NT])
        xn = sb("xn", [P, NT, D])
        xn_t = sb("xn_t", [P, CHUNK])
        logits = sb("logits", [P, NT, EXPERTS])
        top = sb("top", [P, NT, 8])
        top_at = sb("top_at", [P, NT, 8], U32)
        top_f = sb("top_f", [P, NT, 2])
        diff = sb("diff", [P, NT])
        ratio = sb("ratio", [P, NT])
        total = sb("total", [P, NT])
        gate_1 = sb("gate_1", [P, NT])
        gate_2 = sb("gate_2", [P, NT])
        pick_1 = sb("pick_1", [P, NT, EXPERTS])
        pick_2 = sb("pick_2", [P, NT, EXPERTS])
        gates3 = sb("gates3", [P, NT, PARTS, EXPERTS])

        xz = sb("xz", [P, 2, 2 * KD, CHUNK])
        up = sb("up", [P, ET, CHUNK])
        hid = sb("hid", [P, 2, ET, CHUNK])
        rest = sb("rest", [SPREAD, CHUNK])
        part = sb("part", [SPREAD, CHUNK], BF16)
        parts = sb("parts", [SPREAD, 2, CHUNK], BF16)
        soft = sb("soft", [P, KD, CHUNK])
        dt = sb("dt", [P, 2, KD, CHUNK])
        dtu = sb("dtu", [P, 2, KD, CHUNK])
        yz = sb("yz", [P, KD, CHUNK])
        out_sb = sb("out_sb", [P, NT, D])

        carry = sb("carry", [P, KD, STATES])
        h_ring = sb("h_ring", [P, KD, H_RING, CHUNK])
        decay_ring = sb("decay_ring", [P, KD, DECAY_RING, CHUNK])
        bx_dve = sb("bx_dve", [P, BX_RING, KD, CHUNK])
        bx_pool = sb("bx_pool", [P, BX_RING, KD, CHUNK])
        b_sb = sb("b_sb", [P, BX_RING, CHUNK])
        c_sb = sb("c_sb", [P, C_RING, CHUNK])
        hc = sb("hc", [P, Y_RING, KD, CHUNK])

        y_ps = pb("y_ps", [P, KD, CHUNK])
        b_ps = [pb(f"b_ps{i}", [P, CHUNK]) for i in range(B_BANKS)]
        c_ps = pb("c_ps", [P, CHUNK])
        job_ps = [pb(f"job_ps{i}", [P, CHUNK]) for i in range(JOB_BANKS)]

        s_first = sem("first_loads")
        s_weights = sem("weights_loaded")
        s_small = sem("small_loaded")
        s_selector = sem("selector_made")
        s_x = [sem("x_even_loaded"), sem("x_odd_loaded")]
        s_res = sem("residual_loaded")
        s_half = sem("minus_half_set")
        s_nobias = sem("gates_bias_zeroed")
        s_aexp = sem("a_exp_done")
        s_a = sem("a_ready")
        s_stats = sem("stats_ready")
        s_vareps = sem("var_eps_ready")
        s_rstd = sem("rstd_ready")
        s_xn = sem("xn_ready")
        s_T = sem("transposed")
        s_xnT = sem("xn_t_ready")
        s_R = sem("logits_done")
        s_logits = sem("logits_read")
        s_diff = sem("diff_ready")
        s_ratio = sem("ratio_ready")
        s_gates = sem("gates_ready")
        s_Z = sem("in_proj_done")
        s_xz = sem("in_proj_read")
        s_A = sem("w1_done")
        s_up = sem("w1_read")
        s_silu = sem("silu_done")
        s_upsilu = sem("up_silu_done")
        s_X = sem("x_dbl_done")
        s_xdbl = sem("x_dbl_read")
        s_p1 = sem("part1_ready")
        s_r1 = sem("rest1_ready")
        s_p2 = sem("part2_ready")
        s_parts = sem("parts_ready")
        s_D = sem("dt_proj_done")
        s_relu = sem("dt_proj_read")
        s_soft = sem("softplus_ready")
        s_dt = sem("dt_ready")
        s_dtu = sem("dtu_ready")
        s_M = sem("w3_done")
        s_hid = sem("hid_ungated")
        s_gated = sem("hid_gated")
        s_Bps = sem("b_spread")
        s_Cps = sem("c_spread")
        s_Gps = sem("gate_spread")
        s_Bsb = sem("b_copied")
        s_Csb = sem("c_copied")
        s_bxd = sem("bx_by_dve")
        s_bxp = sem("bx_by_pool")
        s_decay = sem("decay_ready")
        s_scan = sem("scanned")
        s_carry = sem("carry_ready")
        s_hc = sem("hc_ready")
        s_sum = sem("summed")
        s_skip = sem("skip_added")
        s_yz = sem("yz_ready")
        s_O = sem("out_proj_done")
        s_resid = sem("residual_biased")
        s_out = sem("out_added")
        s_sent = sem("out_sent")
        s_dve = sem("dve_step")
        s_act = sem("act_step")

        block = ctx.enter_context(nc.Block())

        def whole_run(eng, main, steps=None, per=0):
            pairs = (CHUNKS - 2) // 2
            main(Chunk(-1))
            main(Chunk(0))
            with eng.Fori(0, pairs) as turn:
                if steps:
                    steps.enter(turn, per)
                main(Chunk(1, turn))
                main(Chunk(2, turn))
                if steps:
                    steps.leave(pairs)
            main(Chunk(CHUNKS - 1))
            main(Chunk(CHUNKS))

        @block.sync
        def _(sp):
            def load_x(c):
                if c.since(2):
                    sp.wait_ge(s_xn, c.count(1, -1))
                sp.dma_start(x_t[:, c.parity], x_v[c.index]).then_inc(s_x[c.parity], 16)

            def rows_in_and_out(c):
                if c.since(1):
                    sp.wait_ge(s_out, c.count(NT, 0))
                    sp.dma_start(out_v[(c + -1).index], out_sb[:]).then_inc(s_sent, 16)
                    sp.wait_ge(s_sent, c.count(16, 0))
                sp.dma_start(x_res[:], x_v[c.index]).then_inc(s_res, 16)

            load_x(Chunk(0))
            sp.dma_start(ident[:], ident_c).then_inc(s_first, 16)
            sp.dma_start(w_r[:], router_w).then_inc(s_first, 16)
            sp.dma_start(w_in[:], W_in).then_inc(s_first, 16)
            sp.dma_start(w1[:, 0:EXPERTS, :], routed_w1.rearrange("e d h -> d e h")).then_inc(s_first, 16)
            sp.dma_start(w1[:, EXPERTS:, :], shared_w1.rearrange("e d h -> d e h")).then_inc(s_first, 16)
            sp.dma_start(w_dt[:], W_dt.rearrange("(k p) n -> p k n", p=P)).then_inc(s_weights, 16)
            load_x(Chunk(1))
            sp.dma_start(w3[:, 0:EXPERTS, :], routed_w3.rearrange("e d h -> d e h")).then_inc(s_weights, 16)
            sp.dma_start(w3[:, EXPERTS:, :], shared_w3.rearrange("e d h -> d e h")).then_inc(s_weights, 16)
            sp.dma_start(w_out[:], W_out.rearrange("(k p) n -> p k n", p=P)).then_inc(s_weights, 16)
            sp.dma_start(w2[:, 0:RT, :], routed_w2.rearrange("(j e) h d -> (e h) j d", e=EPT)).then_inc(s_weights, 16)
            sp.dma_start(w2[:, RT, :], shared_w2.rearrange("e h d -> (e h) d")).then_inc(s_weights, 16)
            load_x(Chunk(2))
            rows_in_and_out(Chunk(0))
            with sp.Fori(0, (CHUNKS - 4) // 2) as turn:
                for k in (1, 2):
                    load_x(Chunk(k + 2, turn))
                    rows_in_and_out(Chunk(k, turn))
            load_x(Chunk(CHUNKS - 1))
            for k in range(CHUNKS - 3, CHUNKS):
                rows_in_and_out(Chunk(k))
            sp.wait_ge(s_out, NT * CHUNKS)
            sp.dma_start(out_v[CHUNKS - 1], out_sb[:]).then_inc(s_sent, 16)
            sp.wait_ge(s_sent, 16 * CHUNKS)

        @block.gpsimd
        def _(pool):
            def inverse_deviation(n):
                pool.wait_ge(s_stats, n.count(1, 1))
                pool.tensor_tensor(var_eps[:], mean_var[:, :, 1], eps[:], ALU.add).then_inc(s_vareps, 1)
                pool.wait_ge(s_vareps, n.count(1, 1))
                pool.tensor_tensor(rstd[:], var_eps[:], minus_half[:], ALU.pow).then_inc(s_rstd, 1)

            def dt_times_u(n):
                pool.wait_ge(s_dt, n.count(KD, KD))
                pool.tensor_tensor(dtu[:, n.parity], dt[:, n.parity], xz[:, n.parity, 0:KD],
                                   ALU.mult).then_inc(s_dtu, 1)

            def residual_plus_bias(c):
                pool.wait_ge(s_res, c.count(16, 16))
                pool.tensor_tensor(x_res[:], x_res[:], bias_out[:].unsqueeze(1).to_broadcast([P, NT, D]),
                                   ALU.add).then_inc(s_resid, 1)

            def bx(c, s):
                k = POOL_B.index(s)
                if k == 0:
                    pool.wait_ge(s_dtu, c.count(1, 1))
                pool.wait_ge(s_Bsb, c.count(len(POOL_B), k + 1))
                before = POOL_B[k - BX_RING]
                if k >= BX_RING:
                    pool.wait_ge(s_scan, c.count(KD * STATES, KD * (before + 1)))
                elif c.since(1):
                    pool.wait_ge(s_scan, c.count(KD * STATES, KD * (before + 1 - STATES)))
                pool.tensor_tensor(bx_pool[:, k % BX_RING], dtu[:, c.parity],
                                   b_sb[:, k % BX_RING].unsqueeze(1).to_broadcast([P, KD, CHUNK]),
                                   ALU.mult).then_inc(s_bxp, 1)

            def h_times_c(c, s):
                pool.wait_ge(s_Csb, c.count(STATES, s + 1))
                pool.wait_ge(s_scan, c.count(KD * STATES, KD * (s + 1)))
                if s >= Y_RING or c.since(1):
                    pool.wait_ge(s_sum, c.count(STATES, s + 1 - Y_RING))
                pool.tensor_tensor(hc[:, s % Y_RING], h_ring[:, :, s % H_RING],
                                   c_sb[:, s % C_RING].unsqueeze(1).to_broadcast([P, KD, CHUNK]),
                                   ALU.mult).then_inc(s_hc, 1)

            def main(c):
                for slot in range(STATES):
                    n = c + 1
                    d, s = at_state(c, slot, BX)
                    if d.real and s in POOL_B:
                        bx(d, s)
                    d, s = at_state(c, slot, TIMES_C)
                    if d.real:
                        h_times_c(d, s)
                    if slot == RSTD and n.real:
                        inverse_deviation(n)
                    if slot == DTU and n.real:
                        dt_times_u(n)
                    if slot == RESIDUAL and (c + -1).real:
                        residual_plus_bias(c + -1)

            pool.memset(minus_half[:], -0.5).then_inc(s_half, 1)
            pool.memset(eps[:], EPS).then_inc(s_half, 1)
            pool.wait_ge(s_half, 2)
            pool.wait_ge(s_small, 16 * N_SMALL)
            whole_run(pool, main)

        @block.scalar
        def _(act):
            steps = Steps()

            def normalised_rows(n):
                act.wait_ge(s_T, n.count(1, 1))
                nc.scalar.copy(xn_t[:], job_ps[BANK["T0"]][:]).then_inc(s_xnT, 1)

            def input_projection(n, m):
                if m == 0 and n.since(2):
                    act.wait_ge(s_yz, n.count(1, -1))
                act.wait_ge(s_Z, n.count(2 * KD, m + 1))
                nc.scalar.activation(xz[:, n.parity, m], job_ps[BANK[f"Z{m}"]][:], ACT.Identity,
                                     bias=bias_in[:, m:m + 1]).then_inc(s_xz, 1)

            def expert_up(n, j):
                act.wait_ge(s_A, n.count(ET, j + 1))
                nc.scalar.copy(up[:, j], job_ps[BANK[f"A{j}"]][:]).then_inc(s_up, 1)

            def first_part(n):
                act.wait_ge(s_X, n.count(1, 1))
                nc.scalar.activation(rest[:], job_ps[BANK["X0"]][0:SPREAD, :], ACT.Identity,
                                     bias=bias_x3[:, 0:1]).then_inc(s_xdbl, 1)
                act.wait_ge(s_xdbl, n.count(1, 1))
                nc.scalar.copy(part[:], rest[:]).then_inc(s_p1, 1)

            def second_part(n):
                act.wait_ge(s_r1, n.count(1, 1))
                nc.scalar.copy(part[:], rest[:]).then_inc(s_p2, 1)

            def softplus_begin(n, k):
                ps = job_ps[BANK[f"D{k}"]]
                act.wait_ge(s_D, n.count(KD, k + 1))
                nc.scalar.activation(soft[:, k], ps[:], ACT.Abs, bias=bias_dt[:, k:k + 1]).then_inc(s_act, 1)
                nc.scalar.activation(dt[:, n.parity, k], ps[:], ACT.Relu, bias=bias_dt[:, k:k + 1]).then_inc(s_relu, 1)

            def softplus_end(n, k):
                act.wait_ge(s_act, steps.next())
                nc.scalar.activation(soft[:, k], soft[:, k], ACT.Exp, scale=-1.0).then_inc(s_act, 1)
                act.wait_ge(s_act, steps.next())
                nc.scalar.activation(soft[:, k], soft[:, k], ACT.Ln, bias=1.0).then_inc(s_soft, 1)

            def silu_xz(n):
                act.wait_ge(s_xz, n.count(2 * KD, 2 * KD))
                nc.scalar.activation(xz[:, n.parity], xz[:, n.parity], ACT.Silu).then_inc(s_silu, 1)
                nc.scalar.preload_act_table_set(EXP_LN_SET)

            def silu_up(n):
                act.wait_ge(s_up, n.count(ET, ET))
                nc.scalar.activation(up[:], up[:], ACT.Silu).then_inc(s_upsilu, 1)
                nc.scalar.preload_act_table_set(EXP_LN_SET)

            def gate_ratio(n):
                act.wait_ge(s_diff, n.count(1, 1))
                nc.scalar.activation(ratio[:], diff[:], ACT.Exp).then_inc(s_ratio, 1)

            def decay(c, s):
                for k in range(KD):
                    if s == 0:
                        act.wait_ge(s_dt, c.count(KD, k + 1))
                    if s >= DECAY_RING or c.since(1):
                        act.wait_ge(s_scan, c.count(KD * STATES, KD * (s - DECAY_RING) + k + 1))
                    nc.scalar.activation(decay_ring[:, k, s % DECAY_RING], dt[:, c.parity, k], ACT.Exp,
                                         scale=a_neg[:, k, s:s + 1]).then_inc(s_decay, 1)

            def copy_c(c, s):
                act.wait_ge(s_Cps, c.count(STATES, s + 1))
                if s >= C_RING or c.since(1):
                    act.wait_ge(s_hc, c.count(STATES, s + 1 - C_RING))
                nc.scalar.copy(c_sb[:, s % C_RING], c_ps[:]).then_inc(s_Csb, 1)

            def copy_b(c, s):
                k = POOL_B.index(s)
                act.wait_ge(s_Bps, c.count(STATES, s + 1))
                if k >= BX_RING or c.since(1):
                    act.wait_ge(s_bxp, c.count(len(POOL_B), k + 1 - BX_RING))
                nc.scalar.copy(b_sb[:, k % BX_RING], b_ps[s % B_BANKS][:]).then_inc(s_Bsb, 1)

            def main(c):
                for slot in range(STATES):
                    n = c + 1
                    if n.real:
                        for job, k in [(job, int(job[1])) for job in JOBS if SLOT.get(job) == slot - 1]:
                            if job[0] == "T":
                                normalised_rows(n)
                            if job[0] == "Z":
                                input_projection(n, k)
                            if job[0] == "A":
                                expert_up(n, k)
                            if job[0] == "X":
                                first_part(n)
                            if job[0] == "D":
                                softplus_begin(n, k)
                        if slot == RATIO:
                            gate_ratio(n)
                    d, s = at_state(c, slot, DECAY)
                    if d.real:
                        decay(d, s)
                    d, s = at_state(c, slot, COPY_C)
                    if d.real:
                        copy_c(d, s)
                    d, s = at_state(c, slot, COPY_B)
                    if d.real and s in POOL_B:
                        copy_b(d, s)
                    if n.real:
                        for k in range(KD):
                            if slot == SLOT[f"D{k}"] + 1:
                                softplus_end(n, k)
                        if slot == PART_2:
                            second_part(n)
                        if slot == SILU_XZ:
                            silu_xz(n)
                        if slot == SILU_UP:
                            silu_up(n)

            small = [
                (a_log[:], A_log.rearrange("(k p) s -> p k s", p=P)),
                (bias_in[:], b_in), (bias_dt[:], b_dt), (d_par[:], D_param),
                (bias_out[:], b_out.rearrange("(a d) -> a d", a=1).to_broadcast([P, D])),
                (bias_r[:], router_b.rearrange("(a d) -> a d", a=1).to_broadcast([P, EXPERTS])),
                (rows[:], rows_c), (part_mask[:], part_mask_c), (iota[:], iota_c), (keep[:], keep_c),
            ]
            small += [(w_x3[:, :, q * BC:(q + 1) * BC], W_x.rearrange("(k p) n -> p k n", p=P)) for q in range(PARTS)]
            small += [(bias_x3[q * BC:(q + 1) * BC, :], b_x.rearrange("(n a) -> n a", a=1)) for q in range(PARTS)]
            assert len(small) == N_SMALL
            for dst, src in small:
                act.dma_start(dst, src).then_inc(s_small, 16)
            nc.scalar.preload_act_table_set(EXP_LN_SET)
            act.wait_ge(s_small, 16 * N_SMALL)
            act.wait_ge(s_nobias, 1)
            nc.scalar.activation(a_neg[:], a_log[:], ACT.Exp).then_inc(s_aexp, 1)
            nc.scalar.copy(selector[:, 0:BC], rows[:, 0:BC].unsqueeze(2).to_broadcast([SPREAD, BC, P])
                           ).then_inc(s_selector, 1)
            nc.scalar.copy(selector[:, BC:].rearrange("r j (e h) -> r (j e) h", e=EPT),
                           rows[:, BC:].unsqueeze(2).to_broadcast([SPREAD, EXPERTS, H])).then_inc(s_selector, 1)
            act.wait_ge(s_a, 1)
            whole_run(act, main, steps, ACT_STEPS)

        @block.vector
        def _(dve):
            V = nc.vector
            steps = Steps()

            def wide(ap):
                return ap.unsqueeze(2).to_broadcast([P, NT, EXPERTS])

            def every_tile(ap):
                return ap.unsqueeze(1).to_broadcast([P, NT, EXPERTS])

            def norm_stats(n):
                loaded = 16 * (n.k // 2 + 1)
                dve.wait_ge(s_x[n.parity], loaded if n.turn is None else n.turn * 16 + loaded)
                for t in range(NT):
                    ins = V.bn_stats(stats[:, t], x_t[:, n.parity, t])
                ins.then_inc(s_dve, 1)
                dve.wait_ge(s_dve, steps.next())
                V.memset(seat[:], 0.0)
                for t in range(NT):
                    ins = V.bn_aggr(mean_var[:, t], stats[:, t])
                ins.then_inc(s_stats, 1)

            def norm_apply(n):
                dve.wait_ge(s_rstd, n.count(1, 1))
                for t in range(NT):
                    ins = V.tensor_scalar(xn[:, t], x_t[:, n.parity, t], mean_var[:, t, 0:1], rstd[:, t:t + 1],
                                          ALU.subtract, ALU.mult)
                ins.then_inc(s_xn, 1)

            def route_top(n):
                dve.wait_ge(s_R, n.count(1, 1))
                V.tensor_tensor(logits[:], job_ps[BANK["R0"]][:, 0:NT * EXPERTS].rearrange("p (t e) -> p t e", t=NT),
                                every_tile(bias_r[:]), ALU.add).then_inc(s_logits, 1)
                dve.wait_ge(s_logits, n.count(1, 1))
                V.memset(seat[:], 0.0)
                for t in range(NT):
                    ins = V.max(top[:, t], logits[:, t])
                ins.then_inc(s_dve, 1)
                dve.wait_ge(s_dve, steps.next())
                V.memset(seat[:], 0.0)
                for t in range(NT):
                    V.max_index(top_at[:, t], top[:, t], logits[:, t])
                V.tensor_tensor(diff[:], top[:, :, 1], top[:, :, 0], ALU.subtract).then_inc(s_diff, 1)

            def route_gates(n):
                dve.wait_ge(s_ratio, n.count(1, 1))
                V.tensor_copy(top_f[:], top_at[:, :, 0:2])
                V.tensor_scalar(total[:], ratio[:], 1.0, None, ALU.add).then_inc(s_dve, 1)
                dve.wait_ge(s_dve, steps.next())
                V.reciprocal(gate_1[:], total[:]).then_inc(s_dve, 1)
                V.tensor_tensor(pick_1[:], every_tile(iota[:]), wide(top_f[:, :, 0]), ALU.is_equal)
                V.tensor_tensor(pick_2[:], every_tile(iota[:]), wide(top_f[:, :, 1]), ALU.is_equal)
                dve.wait_ge(s_dve, steps.next())
                V.tensor_tensor(gate_2[:], ratio[:], gate_1[:], ALU.mult).then_inc(s_dve, 1)
                dve.wait_ge(s_dve, steps.next())
                V.tensor_tensor(pick_1[:], pick_1[:], wide(gate_1[:]), ALU.mult)
                V.tensor_tensor(pick_2[:], pick_2[:], wide(gate_2[:]), ALU.mult).then_inc(s_dve, 1)
                dve.wait_ge(s_dve, steps.next())
                for q in range(PARTS):
                    ins = V.tensor_tensor(gates3[:, :, q], pick_1[:], pick_2[:], ALU.add)
                ins.then_inc(s_gates, 1)

            def take_part_1(n):
                dve.wait_ge(s_p1, n.count(1, 1))
                V.scalar_tensor_tensor(rest[:], part[:], part_mask[:, 0:1], rest[:], ALU.mult, ALU.add).then_inc(s_r1, 1)

            def take_part_2(n):
                dve.wait_ge(s_p2, n.count(1, 1))
                V.scalar_tensor_tensor(parts[:, n.parity], part[:], part_mask[:, 1:2], rest[:],
                                       ALU.mult, ALU.add).then_inc(s_parts, 1)

            def softplus_sum(n, k):
                dve.wait_ge(s_soft, n.count(KD, k + 1))
                V.tensor_tensor(dt[:, n.parity, k], dt[:, n.parity, k], soft[:, k], ALU.add).then_inc(s_dt, 1)

            def hidden(n, j):
                if j == 0:
                    dve.wait_ge(s_upsilu, n.count(1, 1))
                dve.wait_ge(s_M, n.count(ET, j + 1))
                V.tensor_tensor(hid[:, n.parity, j], job_ps[BANK[f"M{j}"]][:], up[:, j], ALU.mult).then_inc(s_hid, 1)

            def gated(n, j):
                dve.wait_ge(s_Gps, n.count(RT, j + 1))
                dve.wait_ge(s_hid, n.count(ET, j + 1))
                V.tensor_tensor(hid[:, n.parity, j], job_ps[BANK[f"G{j}"]][:], hid[:, n.parity, j],
                                ALU.mult).then_inc(s_gated, 1)

            def bx(c, s):
                k = DVE_B.index(s)
                if k == 0:
                    dve.wait_ge(s_dtu, c.count(1, 1))
                dve.wait_ge(s_Bps, c.count(STATES, s + 1))
                before = DVE_B[k - BX_RING]
                if k >= BX_RING:
                    dve.wait_ge(s_scan, c.count(KD * STATES, KD * (before + 1)))
                elif c.since(1):
                    dve.wait_ge(s_scan, c.count(KD * STATES, KD * (before + 1 - STATES)))
                V.tensor_tensor(bx_dve[:, k % BX_RING], b_ps[s % B_BANKS][:].unsqueeze(1).to_broadcast([P, KD, CHUNK]),
                                dtu[:, c.parity], ALU.mult).then_inc(s_bxd, 1)

            def scan(c, s):
                if s in POOL_B:
                    k, src = POOL_B.index(s), bx_pool
                    dve.wait_ge(s_bxp, c.count(len(POOL_B), k + 1))
                else:
                    k, src = DVE_B.index(s), bx_dve
                    dve.wait_ge(s_bxd, c.count(len(DVE_B), k + 1))
                if s % H_RING == 0:
                    extra = 0 if c.turn is None and c.k == CHUNKS - 1 else s // H_RING
                    dve.wait_ge(s_carry, c.count(STATES // H_RING, 1 + extra))
                if s >= H_RING or c.since(1):
                    dve.wait_ge(s_hc, c.count(STATES, s + 1 - H_RING))
                for d in range(KD):
                    dve.wait_ge(s_decay, c.count(KD * STATES, KD * s + d + 1))
                    V.tensor_tensor_scan(h_ring[:, d, s % H_RING], decay_ring[:, d, s % DECAY_RING], src[:, k % BX_RING, d],
                                         carry[:, d, s:s + 1], ALU.mult, ALU.add).then_inc(s_scan, 1)

            def keep_carry(c, s):
                dve.wait_ge(s_scan, c.count(KD * STATES, KD * (s + 1)))
                following = (c + 1).index
                V.tensor_scalar(carry[:, :, s + 1 - H_RING:s + 1], h_ring[:, :, :, CHUNK - 1],
                                keep[:, 0, bass.ds(following, 1)], keep[:, 1, bass.ds(following, 1)],
                                ALU.max, ALU.min).then_inc(s_carry, 1)

            def add_skip(c):
                dve.wait_ge(s_sum, c.count(STATES, STATES))
                for k in range(KD):
                    V.scalar_tensor_tensor(yz[:, k], xz[:, c.parity, k], d_par[:, k:k + 1], y_ps[:, k],
                                           ALU.mult, ALU.add).then_inc(s_skip, 1)

            def finish_y(c):
                dve.wait_ge(s_skip, c.count(KD, KD))
                V.tensor_tensor(yz[:], yz[:], xz[:, c.parity, KD:], ALU.mult).then_inc(s_yz, 1)

            def add_residual(c, t):
                dve.wait_ge(s_O, c.count(NT, t + 1))
                if t == 0:
                    dve.wait_ge(s_resid, c.count(1, 1))
                V.tensor_tensor(out_sb[:, t], job_ps[BANK[f"O{t}"]][:, 0:D], x_res[:, t], ALU.add).then_inc(s_out, 1)

            def front(n, slot):
                if slot == TOP2:
                    route_top(n)
                if slot == GATES:
                    route_gates(n)
                if slot == REST_1:
                    take_part_1(n)
                if slot == REST_2:
                    take_part_2(n)
                for job, k in [(job, int(job[1])) for job in JOBS if SLOT.get(job) == slot - 1]:
                    if job[0] == "M":
                        hidden(n, k)
                    if job[0] == "G":
                        gated(n, k)
                for k in range(KD):
                    if slot == SLOT[f"D{k}"] + 2:
                        softplus_sum(n, k)

            def main(c):
                for slot in range(STATES):
                    n = c + 1
                    if slot == STATS and n.real:
                        norm_stats(n)
                    d, s = at_state(c, slot, BX)
                    if d.real and s in DVE_B:
                        bx(d, s)
                    if c.real:
                        scan(c, slot)
                        if (slot + 1) % H_RING == 0 and n.real:
                            keep_carry(c, slot)
                        front(c, slot + STATES)
                    if slot == NORM and n.real:
                        norm_apply(n)
                    if slot == SKIP and (c + -1).real:
                        add_skip(c + -1)
                    if slot == FINISH_Y and (c + -1).real:
                        finish_y(c + -1)
                    for t in range(NT):
                        if slot == SLOT[f"O{t}"] + 1 and (c + -1).real:
                            add_residual(c + -1, t)
                    if n.real:
                        front(n, slot)
            V.memset(bias_x3[PARTS * BC:SPREAD, :], 0.0).then_inc(s_nobias, 1)
            V.memset(carry[:], 0.0).then_inc(s_carry, 1)
            dve.wait_ge(s_aexp, 1)
            V.tensor_scalar(a_neg[:], a_neg[:], -1.0, None, ALU.mult).then_inc(s_a, 1)
            whole_run(dve, main, steps, DVE_STEPS)

        @block.tensor
        def _(pe):
            mm = nc.tensor.matmul

            def bank_for(n, job):
                found = job_before(n, job)
                if found:
                    m, before = found
                    kind, j = before[0], int(before[1])
                    if kind == "T":
                        pe.wait_ge(s_xnT, m.count(1, 1))
                    elif kind == "R":
                        pe.wait_ge(s_logits, m.count(1, 1))
                    elif kind == "Z":
                        pe.wait_ge(s_xz, m.count(2 * KD, j + 1))
                    elif kind == "A":
                        pe.wait_ge(s_up, m.count(ET, j + 1))
                    elif kind == "O":
                        pe.wait_ge(s_out, m.count(NT, j + 1 - 2 * NT))
                    elif kind == "X":
                        pe.wait_ge(s_xdbl, m.count(1, 1))
                    elif kind == "D":
                        pe.wait_ge(s_relu, m.count(KD, j + 1))
                    elif kind == "M":
                        pe.wait_ge(s_hid, m.count(ET, j + 1))
                    elif kind == "G":
                        pe.wait_ge(s_gated, m.count(RT, j + 1))
                return job_ps[BANK[job]]

            def project_out(c, t, ps):
                if t == 0:
                    pe.wait_ge(s_gated, c.count(RT, RT))
                    pe.wait_ge(s_hid, c.count(ET, ET))
                    pe.wait_ge(s_yz, c.count(1, 1))
                tile = slice(t * P, (t + 1) * P)
                for j in range(ET):
                    mm(ps[:, 0:D], hid[:, c.parity, j, tile], w2[:, j], start=(j == 0), stop=False)
                for k in range(KD):
                    ins = mm(ps[:, 0:D], yz[:, k, tile], w_out[:, k], start=False, stop=(k == KD - 1))
                ins.then_inc(s_O, 1)

            def front_job(n, job):
                ps = bank_for(n, job)
                u = xz[:, n.parity]
                kind, j = job[0], int(job[1])
                if kind == "T":
                    pe.wait_ge(s_xn, n.count(1, 1))
                    for t in range(NT):
                        ins = nc.tensor.transpose(ps[:, t * P:(t + 1) * P], xn[:, t], ident[:])
                    ins.then_inc(s_T, 1)
                if kind == "R":
                    pe.wait_ge(s_xnT, n.count(1, 1))
                    for t in range(NT):
                        ins = mm(ps[:, t * EXPERTS:(t + 1) * EXPERTS], xn_t[:, t * P:(t + 1) * P], w_r[:],
                                 start=True, stop=True)
                    ins.then_inc(s_R, 1)
                if kind == "Z":
                    mm(ps[:], w_in[:, j * P:(j + 1) * P], xn_t[:], start=True, stop=True).then_inc(s_Z, 1)
                if kind == "A":
                    mm(ps[:], w1[:, EPT * j:EPT * (j + 1)], xn_t[:], start=True, stop=True).then_inc(s_A, 1)
                if kind == "O":
                    project_out(n + -2, j, ps)
                if kind == "X":
                    pe.wait_ge(s_silu, n.count(1, 1))
                    pe.wait_ge(s_gates, n.count(1, 1))
                    for k in range(KD):
                        mm(ps[0:PARTS * BC, :], w_x3[:, k], u[:, k], start=(k == 0), stop=(k == KD - 1))
                    for t in range(NT):
                        ins = mm(ps[PARTS * BC:SPREAD, t * P:(t + 1) * P],
                                 gates3[:, t].rearrange("p q e -> p (q e)"), ident[:], start=True, stop=True)
                    ins.then_inc(s_X, 1)
                if kind == "D":
                    for k in range(KD):
                        ins = mm(ps[:], w_dt[:, k, j * P:(j + 1) * P], u[:, k], start=(k == 0), stop=(k == KD - 1))
                    ins.then_inc(s_D, 1)
                if kind == "M":
                    mm(ps[:], w3[:, EPT * j:EPT * (j + 1)], xn_t[:], start=True, stop=True).then_inc(s_M, 1)
                if kind == "G":
                    pe.wait_ge(s_parts, n.count(1, 1))
                    mm(ps[:], selector[:, BC + j], parts[:, n.parity], start=True, stop=True).then_inc(s_Gps, 1)

            def spread_b(c, s):
                if s == 0:
                    pe.wait_ge(s_parts, c.count(1, 1))
                if s >= B_BANKS or c.since(1):
                    before, chunks = (s - B_BANKS) % STATES, 0 if s >= B_BANKS else -1
                    if before in POOL_B:
                        pe.wait_ge(s_Bsb, (c + chunks).count(len(POOL_B), POOL_B.index(before) + 1))
                    else:
                        pe.wait_ge(s_bxd, (c + chunks).count(len(DVE_B), DVE_B.index(before) + 1))
                mm(b_ps[s % B_BANKS][:], selector[:, s], parts[:, c.parity], start=True, stop=True).then_inc(s_Bps, 1)

            def spread_c(c, s):
                if s > 0 or c.since(1):
                    pe.wait_ge(s_Csb, c.count(STATES, s))
                mm(c_ps[:], selector[:, STATES + s], parts[:, c.parity], start=True, stop=True).then_inc(s_Cps, 1)

            def sum_states(c, s):
                pe.wait_ge(s_hc, c.count(STATES, s + 1))
                if s == 0 and c.since(1):
                    pe.wait_ge(s_skip, c.count(KD, 0))
                for d in range(KD):
                    ins = mm(y_ps[:, d], ident[:], hc[:, s % Y_RING, d], start=(s == 0), stop=(s == STATES - 1))
                ins.then_inc(s_sum, 1)

            def jobs(n, slot):
                for job in JOBS:
                    if SLOT.get(job) == slot and job_lives(n, job):
                        front_job(n, job)

            def main(c):
                for slot in range(STATES):
                    d, s = at_state(c, slot, SPREAD_B)
                    if d.real:
                        spread_b(d, s)
                    d, s = at_state(c, slot, SPREAD_C)
                    if d.real:
                        spread_c(d, s)
                    d, s = at_state(c, slot, SUM)
                    if slot == SKIP:
                        jobs(c + 1, slot)
                    if d.real:
                        sum_states(d, s)
                    if slot != SKIP:
                        jobs(c + 1, slot)

            pe.wait_ge(s_first, 16 * N_FIRST)
            pe.wait_ge(s_small, 16 * N_SMALL)
            pe.wait_ge(s_weights, 16 * N_WEIGHTS)
            pe.wait_ge(s_selector, 2)
            whole_run(pe, main)


_INS = ["L0_attn_x", "L0_attn_W_in", "L0_attn_b_in", "L0_attn_W_x", "L0_attn_b_x", "L0_attn_W_dt", "L0_attn_b_dt",
        "L0_attn_W_out", "L0_attn_b_out", "L0_attn_A_log", "L0_attn_D_param", "L0_ffn_router_w", "L0_ffn_router_b",
        "L0_ffn_routed_w1", "L0_ffn_routed_w3", "L0_ffn_routed_w2", "L0_ffn_shared_w1", "L0_ffn_shared_w3",
        "L0_ffn_shared_w2"]


def _constants(np):
    rows = np.zeros((SPREAD, BC + EXPERTS), np.float32)
    mask = np.zeros((SPREAD, 2), np.float32)
    for q in range(PARTS):
        for i in range(BC):
            rows[q * BC + i, i] = 1
        for e in range(EXPERTS):
            rows[PARTS * BC + q * EXPERTS + e, BC + e] = 1
        for r in (slice(q * BC, (q + 1) * BC), slice(PARTS * BC + q * EXPERTS, PARTS * BC + (q + 1) * EXPERTS)):
            mask[r, 0] = -1.0 if q >= 1 else 0.0
            mask[r, 1] = -1.0 if q >= 2 else 0.0
    keep = np.zeros((P, 2, CHUNKS), np.float32)
    for c in range(CHUNKS):
        if c % CPB:
            keep[:, 0, c], keep[:, 1, c] = -BIG, BIG
    iota = np.tile(np.arange(EXPERTS, dtype=np.float32), (P, 1))
    return [("ident", np.eye(P, dtype=np.float32)), ("rows", rows), ("part_mask", mask), ("iota", iota),
            ("keep", keep)]


def kernel(**inputs):
    import numpy as _np
    import concourse.bacc as _bacc
    from concourse.bass_utils import run_bass_kernel_spmd as _run

    nc = _bacc.Bacc("TRN2", target_bir_lowering=False, num_devices=1)
    arrays, args = {}, []
    data = {n: _np.asarray(inputs[n]) for n in _INS}
    for n in ("L0_attn_b_in", "L0_attn_b_dt", "L0_attn_D_param"):
        data[n] = data[n].reshape(-1, P).T
    for name, a in list(data.items()) + _constants(_np):
        a = _np.ascontiguousarray(a)
        arrays[f"in_{name}_dram"] = a
        args.append(nc.dram_tensor(f"in_{name}_dram", a.shape, mybir.dt.from_np(a.dtype), kind="ExternalInput").ap())
    args.append(nc.dram_tensor("out_dram", (BATCH, SEQ, D), F32, kind="ExternalOutput").ap())
    mixed_layer_program(nc, *args)
    r = _run(nc, [arrays], core_ids=[0])
    return r.results[0]["out_dram"]
```

```python
import concourse.bass as bass
from concourse import mybir
from contextlib import ExitStack

F32 = mybir.dt.float32
BF16 = mybir.dt.bfloat16
U32 = mybir.dt.uint32
ALU = mybir.AluOpType
ACT = mybir.ActivationFunctionType
EXP_LN_SET = "natural_log_exp_and_others"

P = 128
BATCH, SEQ, D = 2, 2048, 128
INNER, STATES = 256, 16
KD = INNER // P
EXPERTS, SHARED, H = 8, 2, 64
EPT = P // H
RT = EXPERTS // EPT
ET = (EXPERTS + SHARED) // EPT
CHUNK = 512
NT = CHUNK // P
CHUNKS = BATCH * SEQ // CHUNK
CPB = SEQ // CHUNK
PARTS = 3
BC = 2 * STATES
SPREAD = PARTS * (BC + EXPERTS)
EPS = 1e-5
BIG = 3.4028234e38

POOL_B = [s for s in range(STATES) if s % 2 == 1]
DVE_B = [s for s in range(STATES) if s not in POOL_B]
ND = len(DVE_B)
C_RING, Y_RING, B_RING, BX_DVE_RING, BX_POOL_RING, H_RING = 4, 4, 4, 2, 4, 8
assert len(POOL_B) % BX_POOL_RING == 0 and len(DVE_B) % BX_DVE_RING == 0
N_FIRST, N_WEIGHTS, N_SMALL = 5, 11, 4 + 2 * PARTS
ACT_STEPS, DVE_STEPS = 2 * 4, 2 * 2

SLOT = {"T0": 4, "R0": 5, "Z0": 6, "Z1": 6, "Z2": 7, "Z3": 7, "A0": 8, "O0": 8, "D0": 9, "A1": 9,
        "D1": 10, "X0": 11, "A2": 12, "O1": 12, "A3": 13, "O2": 13, "A4": 14, "O3": 14, "M0": 15,
        "M1": 16, "G0": 16, "M2": 17, "G1": 17, "M3": 18, "G2": 18, "M4": 19, "G3": 19}
JOBS = list(SLOT)
JOB_BANKS = 3
while len(JOBS) % JOB_BANKS:
    JOBS.append("--")
BANK = {job: i % JOB_BANKS for i, job in enumerate(JOBS)}
LOAD_B, SPREAD_B, BX, DECAY, SCAN, LOAD_C, TIMES_C, SUM = 2, 1, 0, -2, -3, -3, -5, -7
STATS, RSTD, NORM, FINISH_Y, TOP2, DIFF, RATIO, TOTAL, GATES = 0, 0, 2, 6, 6, 6, 8, 9, 9
SILU_XZ, DTU, SAVE_BC, REST_1, PART_2, REST_2, SILU_UP, RESIDUAL = 8, 12, 13, 13, 14, 14, 15, 7
LOAD_X, LOAD_RESIDUAL, SEND = 3, 0, 15


class Chunk:

    def __init__(self, k, turn=None):
        self.k, self.turn, self.parity = k, turn, k % 2

    def __add__(self, d):
        return Chunk(self.k + d, self.turn)

    def count(self, per, more):
        v = per * self.k + more
        return v if self.turn is None else self.turn * (2 * per) + v

    @property
    def index(self):
        return self.count(1, 0)

    def since(self, k):
        return self.turn is not None or self.k >= k

    @property
    def first(self):
        return self.turn is None and self.k == 0

    @property
    def real(self):
        return self.turn is not None or 0 <= self.k < CHUNKS


class Steps:

    def __init__(self):
        self.n, self.turn, self.per = 0, None, 0

    def next(self):
        self.n += 1
        return self.n if self.turn is None else self.turn * self.per + self.n

    def enter(self, turn, per):
        self.turn, self.per, self.base = turn, per, self.n

    def leave(self, turns):
        assert self.n - self.base == self.per, (self.n - self.base, self.per)
        self.n, self.turn = self.base + turns * self.per, None


def job_before(n, job):
    i = JOBS.index(job) - JOB_BANKS
    while True:
        m = n if i >= 0 else n + -1
        before = JOBS[i % len(JOBS)]
        if before == "--" or not job_lives(m, before):
            i -= JOB_BANKS
            if m.turn is None and m.k < 0:
                return None
            if i < -len(JOBS):
                return None
            continue
        return m, before


def job_lives(n, job):
    return n.turn is not None or (0 <= n.k - 2 < CHUNKS if job[0] == "O" else n.real)


def at_state(c, slot, ahead):
    return c + (slot + ahead) // STATES, (slot + ahead) % STATES


def mixed_layer_program(nc, x, W_in, b_in, W_x, b_x, W_dt, b_dt, W_out, b_out, A_log, D_param,
                        router_w, router_b, routed_w1, routed_w3, routed_w2,
                        shared_w1, shared_w3, shared_w2, ident_c, rows_c, part_mask_c, iota_c, keep_c, bc_rows, out):
    x_v = x.rearrange("b s d -> (b s) d").rearrange("(c n p) d -> c p n d", n=NT, p=P)
    out_v = out.rearrange("b s d -> (b s) d").rearrange("(c n p) d -> c p n d", n=NT, p=P)
    ctx = ExitStack()
    with ctx:
        def sb(name, shape, dt=F32):
            return ctx.enter_context(nc.sbuf_tensor(name, shape, dt))

        def pb(name, shape):
            return ctx.enter_context(nc.psum_tensor(name, shape, F32))

        def sem(name):
            return ctx.enter_context(nc.semaphore(name))

        w_in = sb("w_in", [P, 2 * INNER])
        w_x3 = sb("w_x3", [P, KD, PARTS * BC])
        w_dt = sb("w_dt", [P, KD, INNER])
        w_out = sb("w_out", [P, KD, D])
        w_r = sb("w_r", [P, EXPERTS])
        w1 = sb("w1", [P, EXPERTS + SHARED, H])
        w3 = sb("w3", [P, EXPERTS + SHARED, H])
        w2 = sb("w2", [P, ET, D])
        bias_in = sb("bias_in", [P, 2 * KD])
        bias_x3 = sb("bias_x3", [SPREAD, 1])
        bias_dt = sb("bias_dt", [P, KD])
        bias_out = sb("bias_out", [P, D])
        bias_r = sb("bias_r", [P, EXPERTS])
        d_par = sb("d_par", [P, KD])
        a_log = sb("a_log", [P, KD, STATES])
        a_neg = sb("a_neg", [P, KD, STATES])
        ident = sb("ident", [P, P])
        selector = sb("selector", [SPREAD, ND + RT, P], BF16)
        rows = sb("rows", [SPREAD, ND + EXPERTS])
        part_mask = sb("part_mask", [SPREAD, 2])
        iota = sb("iota", [P, EXPERTS])
        keep = sb("keep", [P, 2, CHUNKS])
        minus_half = sb("minus_half", [P, NT])
        minus_one = sb("minus_one", [P, NT])
        eps = sb("eps", [P, NT])
        seat = sb("seat", [P, 1])

        x_t = sb("x_t", [P, 2, NT, D])
        x_res = sb("x_res", [P, NT, D])
        stats = sb("stats", [P, NT, 6])
        mean_var = sb("mean_var", [P, NT, 2])
        var_eps = sb("var_eps", [P, NT])
        rstd = sb("rstd", [P, NT])
        minus_mean = sb("minus_mean", [P, NT])
        shift = sb("shift", [P, NT])
        xn = sb("xn", [P, NT, D])
        xn_t = sb("xn_t", [P, CHUNK])
        logits = sb("logits", [P, NT, EXPERTS])
        top = sb("top", [P, NT, 8])
        top_at = sb("top_at", [P, NT, 8], U32)
        top_f = sb("top_f", [P, NT, 2])
        diff = sb("diff", [P, NT])
        ratio = sb("ratio", [P, NT])
        total = sb("total", [P, NT])
        gate = sb("gate", [P, NT, 2])
        pick = sb("pick", [P, NT, 2, EXPERTS])
        gates3 = sb("gates3", [P, NT, PARTS, EXPERTS])

        xz = sb("xz", [P, 2, 2 * KD, CHUNK])
        up = sb("up", [P, ET, CHUNK])
        hid = sb("hid", [P, 2, ET, CHUNK])
        rest = sb("rest", [SPREAD, CHUNK])
        part = sb("part", [SPREAD, CHUNK], BF16)
        parts = sb("parts", [SPREAD, 2, CHUNK], BF16)
        soft = sb("soft", [P, KD, CHUNK])
        dt = sb("dt", [P, 2, KD, CHUNK])
        dtu = sb("dtu", [P, 2, KD, CHUNK])
        yz = sb("yz", [P, KD, CHUNK])
        out_sb = sb("out_sb", [P, NT, D])

        carry = sb("carry", [P, KD, STATES])
        h_ring = sb("h_ring", [P, KD, H_RING, CHUNK])
        bx_dve = sb("bx_dve", [P, BX_DVE_RING, KD, CHUNK])
        bx_pool = sb("bx_pool", [P, BX_POOL_RING, KD, CHUNK])
        b_sb = sb("b_sb", [P, B_RING, CHUNK])
        c_sb = sb("c_sb", [P, C_RING, CHUNK])
        hc = sb("hc", [P, Y_RING, KD, CHUNK])

        y_ps = pb("y_ps", [P, KD, CHUNK])
        decay_ps = pb("decay_ps", [P, KD, CHUNK])
        b_ps = pb("b_ps", [P, CHUNK])
        job_ps = [pb(f"job_ps{i}", [P, CHUNK]) for i in range(JOB_BANKS)]

        s_ident = sem("identity_loaded")
        s_first = sem("first_loads")
        s_weights = sem("weights_loaded")
        s_small = sem("small_loaded")
        s_selector = sem("selector_made")
        s_x = [sem("x_even_loaded"), sem("x_odd_loaded")]
        s_res = sem("residual_loaded")
        s_half = sem("minus_half_set")
        s_nobias = sem("gates_bias_zeroed")
        s_a = sem("a_ready")
        s_stats = sem("stats_ready")
        s_vareps = sem("var_eps_ready")
        s_rstd = sem("rstd_ready")
        s_shift = sem("shift_ready")
        s_xn = sem("xn_ready")
        s_T = sem("transposed")
        s_xnT = sem("xn_t_ready")
        s_R = sem("logits_done")
        s_logits = sem("logits_read")
        s_diff = sem("diff_ready")
        s_top = sem("top_two_found")
        s_ratio = sem("ratio_ready")
        s_total = sem("total_ready")
        s_gate1 = sem("gate_1_ready")
        s_gate2 = sem("gate_2_ready")
        s_pick = sem("picks_weighted")
        s_gates = sem("gates_ready")
        s_Z = sem("in_proj_done")
        s_xz = sem("in_proj_read")
        s_A = sem("w1_done")
        s_up = sem("w1_read")
        s_silu = sem("silu_done")
        s_upsilu = sem("up_silu_done")
        s_X = sem("x_dbl_done")
        s_xdbl = sem("x_dbl_read")
        s_p1 = sem("part1_ready")
        s_r1 = sem("rest1_ready")
        s_p2 = sem("part2_ready")
        s_parts = sem("parts_ready")
        s_D = sem("dt_proj_done")
        s_relu = sem("dt_proj_read")
        s_soft = sem("softplus_ready")
        s_dt = sem("dt_ready")
        s_dtu = sem("dtu_ready")
        s_M = sem("w3_done")
        s_hid = sem("hid_ungated")
        s_gated = sem("hid_gated")
        s_Bps = sem("b_spread")
        s_Gps = sem("gate_spread")
        s_saved = sem("bc_saved")
        s_Bsb = [sem(f"b_loaded_{i}") for i in range(B_RING)]
        s_Csb = [sem(f"c_loaded_{i}") for i in range(C_RING)]
        s_bxd = sem("bx_by_dve")
        s_bxp = sem("bx_by_pool")
        s_decay = sem("decay_ready")
        s_scan = sem("scanned")
        s_carry = sem("carry_ready")
        s_hc = sem("hc_ready")
        s_sum = sem("summed")
        s_skip = sem("skip_added")
        s_yz = sem("yz_ready")
        s_O = sem("out_proj_done")
        s_resid = sem("residual_biased")
        s_out = sem("out_added")
        s_sent = sem("out_sent")
        s_dve = sem("dve_step")
        s_act = sem("act_step")

        block = ctx.enter_context(nc.Block())

        def whole_run(eng, main, steps=None, per=0, first=1, last=CHUNKS - 2):
            chunks = [Chunk(k) for k in range(-1, CHUNKS + 1)]
            pairs = (last - first + 1) // 2
            for c in chunks[:first + 1]:
                main(c)
            with eng.Fori(0, pairs) as turn:
                if steps:
                    steps.enter(turn, per)
                main(Chunk(first, turn))
                main(Chunk(first + 1, turn))
                if steps:
                    steps.leave(pairs)
            for c in chunks[last + 2:]:
                main(c)

        @block.sync
        def _(sp):
            def load_x(c):
                if c.since(2):
                    sp.wait_ge(s_xn, c.count(1, -1))
                sp.dma_start(x_t[:, c.parity], x_v[c.index]).then_inc(s_x[c.parity], 16)

            def load_residual(c):
                if c.since(1):
                    sp.wait_ge(s_sent, c.count(16, 0))
                sp.dma_start(x_res[:], x_v[c.index]).then_inc(s_res, 16)

            def send(c):
                sp.wait_ge(s_out, c.count(NT, NT))
                sp.dma_start(out_v[c.index], out_sb[:]).then_inc(s_sent, 16)

            def save_bc(n):
                sp.wait_ge(s_xdbl, n.count(1, 1))
                sp.dma_start(bc_rows[n.parity], rest[0:BC, :]).then_inc(s_saved, 16)

            def load_b(c, s):
                k = POOL_B.index(s)
                if k == 0 and c.turn is None:
                    sp.wait_ge(s_saved, c.count(16, 16))
                if k >= B_RING or c.since(1):
                    sp.wait_ge(s_bxp, c.count(len(POOL_B), k + 1 - B_RING))
                sp.dma_start(b_sb[:, k % B_RING], bc_rows[c.parity, s:s + 1, :].to_broadcast([P, CHUNK])
                             ).then_inc(s_Bsb[k % B_RING], 16)

            def load_c(c, s):
                if s >= C_RING or c.since(1):
                    sp.wait_ge(s_hc, c.count(STATES, s + 1 - C_RING))
                sp.dma_start(c_sb[:, s % C_RING],
                             bc_rows[c.parity, STATES + s:STATES + s + 1, :].to_broadcast([P, CHUNK])
                             ).then_inc(s_Csb[s % C_RING], 16)

            def main(c):
                n = c + 1
                for slot in range(STATES):
                    if slot == SEND and (c + -1).real:
                        send(c + -1)
                    d, s = at_state(c, slot, LOAD_B)
                    if d.real and s in POOL_B:
                        load_b(d, s)
                    d, s = at_state(c, slot, LOAD_C)
                    if d.real:
                        load_c(d, s)
                    if slot == SAVE_BC and n.real:
                        save_bc(n)
                    if slot == LOAD_X and (n + 1).real and (n + 1).since(2):
                        load_x(n + 1)
                    if slot == LOAD_RESIDUAL and (c + -1).real:
                        load_residual(c + -1)

            load_x(Chunk(0))
            sp.dma_start(ident[:], ident_c).then_inc(s_ident, 16)
            for dst, src in [
                (w_r[:], router_w), (w_in[:], W_in), (iota[:], iota_c),
                (w1[:, 0:EXPERTS, :], routed_w1.rearrange("e d h -> d e h")),
                (w1[:, EXPERTS:, :], shared_w1.rearrange("e d h -> d e h")),
            ]:
                sp.dma_start(dst, src).then_inc(s_first, 16)
            for dst, src in [
                (rows[:], rows_c), (part_mask[:], part_mask_c),
                (w_dt[:], W_dt.rearrange("(k p) n -> p k n", p=P)),
                (w3[:, 0:EXPERTS, :], routed_w3.rearrange("e d h -> d e h")),
                (w3[:, EXPERTS:, :], shared_w3.rearrange("e d h -> d e h")),
                (keep[:], keep_c), (d_par[:], D_param),
                (bias_out[:], b_out.rearrange("(a d) -> a d", a=1).to_broadcast([P, D])),
                (w_out[:], W_out.rearrange("(k p) n -> p k n", p=P)),
                (w2[:, 0:RT, :], routed_w2.rearrange("(j e) h d -> (e h) j d", e=EPT)),
                (w2[:, RT, :], shared_w2.rearrange("e h d -> (e h) d")),
            ]:
                sp.dma_start(dst, src).then_inc(s_weights, 16)
            load_x(Chunk(1))
            whole_run(sp, main, first=2, last=CHUNKS - 3)
            sp.wait_ge(s_sent, 16 * CHUNKS)
            sp.wait_ge(s_saved, 16 * CHUNKS)

        @block.gpsimd
        def _(pool):
            def inverse_deviation(n):
                pool.wait_ge(s_stats, n.count(1, 1))
                pool.tensor_tensor(minus_mean[:], mean_var[:, :, 0], minus_one[:], ALU.mult)
                pool.tensor_tensor(var_eps[:], mean_var[:, :, 1], eps[:], ALU.add).then_inc(s_vareps, 1)
                pool.wait_ge(s_vareps, n.count(1, 1))
                pool.tensor_tensor(rstd[:], var_eps[:], minus_half[:], ALU.pow).then_inc(s_rstd, 1)
                pool.wait_ge(s_rstd, n.count(1, 1))
                pool.tensor_tensor(shift[:], minus_mean[:], rstd[:], ALU.mult).then_inc(s_shift, 1)

            def wide(ap):
                return ap.unsqueeze(3).to_broadcast([P, NT, 2, EXPERTS])

            def second_less_first(n):
                pool.wait_ge(s_top, n.count(1, 1))
                pool.tensor_tensor(diff[:], top[:, :, 1], top[:, :, 0], ALU.subtract).then_inc(s_diff, 1)
                pool.tensor_copy(top_f[:], top_at[:, :, 0:2]).then_inc(s_diff, 1)

            def gates(n):
                pool.wait_ge(s_gate1, n.count(1, 1))
                pool.tensor_tensor(gate[:, :, 1], ratio[:], gate[:, :, 0], ALU.mult).then_inc(s_gate2, 1)
                pool.wait_ge(s_gate2, n.count(1, 1))
                pool.tensor_tensor(pick[:], pick[:], wide(gate[:]), ALU.mult).then_inc(s_pick, 1)
                pool.wait_ge(s_pick, n.count(1, 1))
                for q in range(PARTS):
                    ins = pool.tensor_tensor(gates3[:, :, q], pick[:, :, 0], pick[:, :, 1], ALU.add)
                ins.then_inc(s_gates, 1)

            def make_selectors():
                pool.wait_ge(s_weights, 16 * N_WEIGHTS)
                pool.tensor_copy(selector[:, 0:ND], rows[:, 0:ND].unsqueeze(2).to_broadcast([SPREAD, ND, P])
                                 ).then_inc(s_selector, 1)
                pool.tensor_copy(selector[:, ND:].rearrange("r j (e h) -> r (j e) h", e=EPT),
                                 rows[:, ND:].unsqueeze(2).to_broadcast([SPREAD, EXPERTS, H])).then_inc(s_selector, 1)

            def dt_times_u(n):
                pool.wait_ge(s_dt, n.count(KD, KD))
                pool.tensor_tensor(dtu[:, n.parity], dt[:, n.parity], xz[:, n.parity, 0:KD],
                                   ALU.mult).then_inc(s_dtu, 1)

            def residual_plus_bias(c):
                pool.wait_ge(s_res, c.count(16, 16))
                pool.tensor_tensor(x_res[:], x_res[:], bias_out[:].unsqueeze(1).to_broadcast([P, NT, D]),
                                   ALU.add).then_inc(s_resid, 1)

            def bx(c, s):
                k = POOL_B.index(s)
                if k == 0:
                    pool.wait_ge(s_dtu, c.count(1, 1))
                loads = len(POOL_B) // B_RING
                pool.wait_ge(s_Bsb[k % B_RING], c.count(16 * loads, 16 * (k // B_RING + 1)))
                before = POOL_B[k - BX_POOL_RING]
                if k >= BX_POOL_RING:
                    pool.wait_ge(s_scan, c.count(KD * STATES, KD * (before + 1)))
                elif c.since(1):
                    pool.wait_ge(s_scan, c.count(KD * STATES, KD * (before + 1 - STATES)))
                pool.tensor_tensor(bx_pool[:, k % BX_POOL_RING], dtu[:, c.parity],
                                   b_sb[:, k % B_RING].unsqueeze(1).to_broadcast([P, KD, CHUNK]),
                                   ALU.mult).then_inc(s_bxp, 1)

            def h_times_c(c, s):
                loads = STATES // C_RING
                pool.wait_ge(s_Csb[s % C_RING], c.count(16 * loads, 16 * (s // C_RING + 1)))
                pool.wait_ge(s_scan, c.count(KD * STATES, KD * (s + 1)))
                if s >= Y_RING or c.since(1):
                    pool.wait_ge(s_sum, c.count(STATES, s + 1 - Y_RING))
                pool.tensor_tensor(hc[:, s % Y_RING], h_ring[:, :, s % H_RING],
                                   c_sb[:, s % C_RING].unsqueeze(1).to_broadcast([P, KD, CHUNK]),
                                   ALU.mult).then_inc(s_hc, 1)

            def main(c):
                for slot in range(STATES):
                    n = c + 1
                    d, s = at_state(c, slot, BX)
                    if d.real and s in POOL_B:
                        bx(d, s)
                    if slot == RSTD and n.real:
                        inverse_deviation(n)
                        if n.first:
                            make_selectors()
                    if slot == DIFF and n.real:
                        second_less_first(n)
                    if slot == GATES and n.real:
                        gates(n)
                    if slot == DTU and n.real:
                        dt_times_u(n)
                    d, s = at_state(c, slot, TIMES_C)
                    if d.real:
                        h_times_c(d, s)
                    if slot == RESIDUAL and (c + -1).real:
                        residual_plus_bias(c + -1)

            pool.memset(minus_half[:], -0.5).then_inc(s_half, 1)
            pool.memset(eps[:], EPS).then_inc(s_half, 1)
            pool.memset(minus_one[:], -1.0).then_inc(s_half, 1)
            pool.wait_ge(s_half, 3)
            whole_run(pool, main)

        @block.scalar
        def _(act):
            steps = Steps()

            def normalise(n):
                act.wait_ge(s_shift, n.count(1, 1))
                for t in range(NT):
                    ins = nc.scalar.activation(xn[:, t], x_t[:, n.parity, t], ACT.Identity,
                                               scale=rstd[:, t:t + 1], bias=shift[:, t:t + 1])
                ins.then_inc(s_xn, 1)

            def transposed_rows(n):
                act.wait_ge(s_T, n.count(1, 1))
                nc.scalar.copy(xn_t[:], job_ps[BANK["T0"]][:]).then_inc(s_xnT, 1)

            def decay_rates():
                act.wait_ge(s_small, 16 * N_SMALL)
                nc.scalar.activation(a_neg[:], a_log[:], ACT.Exp).then_inc(s_a, 1)
                act.wait_ge(s_a, 1)
                nc.scalar.activation(a_neg[:], a_neg[:], ACT.Copy, scale=-1.0).then_inc(s_a, 1)

            def input_projection(n, m):
                if m == 0 and n.since(2):
                    act.wait_ge(s_yz, n.count(1, -1))
                if m == 0 and n.first:
                    decay_rates()
                act.wait_ge(s_Z, n.count(2 * KD, m + 1))
                nc.scalar.activation(xz[:, n.parity, m], job_ps[BANK[f"Z{m}"]][:], ACT.Identity,
                                     bias=bias_in[:, m:m + 1]).then_inc(s_xz, 1)

            def expert_up(n, j):
                act.wait_ge(s_A, n.count(ET, j + 1))
                nc.scalar.copy(up[:, j], job_ps[BANK[f"A{j}"]][:]).then_inc(s_up, 1)

            def first_part(n):
                if n.first:
                    act.wait_ge(s_nobias, 1)
                act.wait_ge(s_X, n.count(1, 1))
                nc.scalar.activation(rest[:], job_ps[BANK["X0"]][0:SPREAD, :], ACT.Identity,
                                     bias=bias_x3[:, 0:1]).then_inc(s_xdbl, 1)
                act.wait_ge(s_xdbl, n.count(1, 1))
                nc.scalar.copy(part[:], rest[:]).then_inc(s_p1, 1)

            def second_part(n):
                act.wait_ge(s_r1, n.count(1, 1))
                nc.scalar.copy(part[:], rest[:]).then_inc(s_p2, 1)

            def softplus_begin(n, k):
                ps = job_ps[BANK[f"D{k}"]]
                act.wait_ge(s_D, n.count(KD, k + 1))
                nc.scalar.activation(soft[:, k], ps[:], ACT.Abs, bias=bias_dt[:, k:k + 1]).then_inc(s_act, 1)
                nc.scalar.activation(dt[:, n.parity, k], ps[:], ACT.Relu, bias=bias_dt[:, k:k + 1]).then_inc(s_relu, 1)

            def softplus_end(n, k):
                act.wait_ge(s_act, steps.next())
                nc.scalar.activation(soft[:, k], soft[:, k], ACT.Exp, scale=-1.0).then_inc(s_act, 1)
                act.wait_ge(s_act, steps.next())
                nc.scalar.activation(soft[:, k], soft[:, k], ACT.Ln, bias=1.0).then_inc(s_soft, 1)

            def silu_xz(n):
                act.wait_ge(s_xz, n.count(2 * KD, 2 * KD))
                nc.scalar.activation(xz[:, n.parity], xz[:, n.parity], ACT.Silu).then_inc(s_silu, 1)
                nc.scalar.preload_act_table_set(EXP_LN_SET)

            def silu_up(n):
                act.wait_ge(s_up, n.count(ET, ET))
                nc.scalar.activation(up[:], up[:], ACT.Silu).then_inc(s_upsilu, 1)
                nc.scalar.preload_act_table_set(EXP_LN_SET)

            def gate_ratio(n):
                act.wait_ge(s_diff, n.count(2, 2))
                nc.scalar.activation(ratio[:], diff[:], ACT.Exp).then_inc(s_ratio, 1)
                act.wait_ge(s_ratio, n.count(1, 1))
                nc.scalar.activation(total[:], ratio[:], ACT.Identity, bias=1.0).then_inc(s_total, 1)

            def decay(c, s):
                if s == 0 and c.first:
                    act.wait_ge(s_a, 2)
                for k in range(KD):
                    if s == 0:
                        act.wait_ge(s_dt, c.count(KD, k + 1))
                    if s > 0 or c.since(1):
                        act.wait_ge(s_scan, c.count(KD * STATES, KD * (s - 1) + k + 1))
                    nc.scalar.activation(decay_ps[:, k], dt[:, c.parity, k], ACT.Exp,
                                         scale=a_neg[:, k, s:s + 1]).then_inc(s_decay, 1)

            def evacuate(n, slot):
                for job in JOBS:
                    k = int(job[1]) if job in SLOT else None
                    if SLOT.get(job) != slot - 1:
                        continue
                    if job[0] == "T":
                        transposed_rows(n)
                    if job[0] == "Z":
                        input_projection(n, k)
                    if job[0] == "A":
                        expert_up(n, k)
                    if job[0] == "X":
                        first_part(n)
                    if job[0] == "D":
                        softplus_begin(n, k)
                        softplus_end(n, k)

            def main(c):
                n = c + 1
                for slot in range(STATES):
                    d, s = at_state(c, slot, DECAY)
                    if d.real:
                        decay(d, s)
                    if n.real:
                        evacuate(n, slot)
                        if slot == NORM:
                            normalise(n)
                        if slot == RATIO:
                            gate_ratio(n)
                        if slot == PART_2:
                            second_part(n)
                        if slot == SILU_XZ:
                            silu_xz(n)
                        if slot == SILU_UP:
                            silu_up(n)

            small = [
                (bias_in[:], b_in),
                (bias_r[:], router_b.rearrange("(a d) -> a d", a=1).to_broadcast([P, EXPERTS])),
            ]
            small += [(w_x3[:, :, q * BC:(q + 1) * BC], W_x.rearrange("(k p) n -> p k n", p=P)) for q in range(PARTS)]
            small += [(bias_x3[q * BC:(q + 1) * BC, :], b_x.rearrange("(n a) -> n a", a=1)) for q in range(PARTS)]
            small += [(bias_dt[:], b_dt), (a_log[:], A_log.rearrange("(k p) s -> p k s", p=P))]
            assert len(small) == N_SMALL
            for dst, src in small:
                act.dma_start(dst, src).then_inc(s_small, 16)
            nc.scalar.preload_act_table_set(EXP_LN_SET)
            whole_run(act, main, steps, ACT_STEPS)

        @block.vector
        def _(dve):
            V = nc.vector
            steps = Steps()

            def every_tile(ap):
                return ap.unsqueeze(1).to_broadcast([P, NT, EXPERTS])

            def norm_stats(n):
                loaded = 16 * (n.k // 2 + 1)
                dve.wait_ge(s_x[n.parity], loaded if n.turn is None else n.turn * 16 + loaded)
                for t in range(NT):
                    ins = V.bn_stats(stats[:, t], x_t[:, n.parity, t])
                ins.then_inc(s_dve, 1)
                dve.wait_ge(s_dve, steps.next())
                V.memset(seat[:], 0.0)
                for t in range(NT):
                    ins = V.bn_aggr(mean_var[:, t], stats[:, t])
                ins.then_inc(s_stats, 1)

            def route_top(n):
                if n.first:
                    dve.wait_ge(s_small, 16 * N_SMALL)
                    dve.wait_ge(s_first, 16 * N_FIRST)
                dve.wait_ge(s_R, n.count(1, 1))
                V.tensor_tensor(logits[:], job_ps[BANK["R0"]][:, 0:NT * EXPERTS].rearrange("p (t e) -> p t e", t=NT),
                                every_tile(bias_r[:]), ALU.add).then_inc(s_logits, 1)
                dve.wait_ge(s_logits, n.count(1, 1))
                V.memset(seat[:], 0.0)
                for t in range(NT):
                    ins = V.max(top[:, t], logits[:, t])
                ins.then_inc(s_dve, 1)
                dve.wait_ge(s_dve, steps.next())
                V.memset(seat[:], 0.0)
                for t in range(NT):
                    ins = V.max_index(top_at[:, t], top[:, t], logits[:, t])
                ins.then_inc(s_top, 1)

            def first_gate(n):
                dve.wait_ge(s_total, n.count(1, 1))
                V.tensor_tensor(pick[:], iota[:].unsqueeze(1).unsqueeze(1).to_broadcast([P, NT, 2, EXPERTS]),
                                top_f[:].unsqueeze(3).to_broadcast([P, NT, 2, EXPERTS]), ALU.is_equal)
                V.reciprocal(gate[:, :, 0], total[:]).then_inc(s_gate1, 1)

            def take_part_1(n):
                if n.first:
                    dve.wait_ge(s_weights, 16 * N_WEIGHTS)
                dve.wait_ge(s_saved, n.count(16, 16))
                dve.wait_ge(s_p1, n.count(1, 1))
                V.scalar_tensor_tensor(rest[:], part[:], part_mask[:, 0:1], rest[:], ALU.mult, ALU.add).then_inc(s_r1, 1)

            def take_part_2(n):
                dve.wait_ge(s_p2, n.count(1, 1))
                V.scalar_tensor_tensor(parts[:, n.parity], part[:], part_mask[:, 1:2], rest[:],
                                       ALU.mult, ALU.add).then_inc(s_parts, 1)

            def softplus_sum(n, k):
                dve.wait_ge(s_soft, n.count(KD, k + 1))
                V.tensor_tensor(dt[:, n.parity, k], dt[:, n.parity, k], soft[:, k], ALU.add).then_inc(s_dt, 1)

            def hidden(n, j):
                if j == 0:
                    dve.wait_ge(s_upsilu, n.count(1, 1))
                dve.wait_ge(s_M, n.count(ET, j + 1))
                V.tensor_tensor(hid[:, n.parity, j], job_ps[BANK[f"M{j}"]][:], up[:, j], ALU.mult).then_inc(s_hid, 1)

            def gated(n, j):
                dve.wait_ge(s_Gps, n.count(RT, j + 1))
                dve.wait_ge(s_hid, n.count(ET, j + 1))
                V.tensor_tensor(hid[:, n.parity, j], job_ps[BANK[f"G{j}"]][:], hid[:, n.parity, j],
                                ALU.mult).then_inc(s_gated, 1)

            def bx(c, s):
                k = DVE_B.index(s)
                if k == 0:
                    dve.wait_ge(s_dtu, c.count(1, 1))
                dve.wait_ge(s_Bps, c.count(len(DVE_B), k + 1))
                before = DVE_B[k - BX_DVE_RING]
                if k >= BX_DVE_RING:
                    dve.wait_ge(s_scan, c.count(KD * STATES, KD * (before + 1)))
                elif c.since(1):
                    dve.wait_ge(s_scan, c.count(KD * STATES, KD * (before + 1 - STATES)))
                V.tensor_tensor(bx_dve[:, k % BX_DVE_RING], b_ps[:].unsqueeze(1).to_broadcast([P, KD, CHUNK]),
                                dtu[:, c.parity], ALU.mult).then_inc(s_bxd, 1)

            def scan(c, s):
                if s in POOL_B:
                    k, src, ring = POOL_B.index(s), bx_pool, BX_POOL_RING
                    dve.wait_ge(s_bxp, c.count(len(POOL_B), k + 1))
                else:
                    k, src, ring = DVE_B.index(s), bx_dve, BX_DVE_RING
                    dve.wait_ge(s_bxd, c.count(len(DVE_B), k + 1))
                if s % H_RING == 0:
                    extra = 0 if c.turn is None and c.k == CHUNKS - 1 else s // H_RING
                    dve.wait_ge(s_carry, c.count(STATES // H_RING, 1 + extra))
                if s >= H_RING or c.since(1):
                    dve.wait_ge(s_hc, c.count(STATES, s + 1 - H_RING))
                for d in range(KD):
                    dve.wait_ge(s_decay, c.count(KD * STATES, KD * s + d + 1))
                    V.tensor_tensor_scan(h_ring[:, d, s % H_RING], decay_ps[:, d], src[:, k % ring, d],
                                         carry[:, d, s:s + 1], ALU.mult, ALU.add).then_inc(s_scan, 1)

            def keep_carry(c, s):
                dve.wait_ge(s_scan, c.count(KD * STATES, KD * (s + 1)))
                following = (c + 1).index
                V.tensor_scalar(carry[:, :, s + 1 - H_RING:s + 1], h_ring[:, :, :, CHUNK - 1],
                                keep[:, 0, bass.ds(following, 1)], keep[:, 1, bass.ds(following, 1)],
                                ALU.max, ALU.min).then_inc(s_carry, 1)

            def finish_y(c):
                dve.wait_ge(s_sum, c.count(STATES, STATES))
                for k in range(KD):
                    V.scalar_tensor_tensor(y_ps[:, k], xz[:, c.parity, k], d_par[:, k:k + 1], y_ps[:, k],
                                           ALU.mult, ALU.add).then_inc(s_skip, 1)
                dve.wait_ge(s_skip, c.count(KD, KD))
                V.tensor_tensor(yz[:], y_ps[:], xz[:, c.parity, KD:], ALU.mult).then_inc(s_yz, 1)

            def add_residual(c, t):
                dve.wait_ge(s_O, c.count(NT, t + 1))
                if t == 0:
                    dve.wait_ge(s_resid, c.count(1, 1))
                V.tensor_tensor(out_sb[:, t], job_ps[BANK[f"O{t}"]][:, 0:D], x_res[:, t], ALU.add).then_inc(s_out, 1)

            def front(n, slot):
                if slot == STATS:
                    norm_stats(n)
                if slot == TOP2:
                    route_top(n)
                if slot == TOTAL:
                    first_gate(n)
                if slot == REST_1:
                    take_part_1(n)
                if slot == REST_2:
                    take_part_2(n)
                for job, k in [(job, int(job[1])) for job in JOBS if SLOT.get(job) == slot - 1]:
                    if job[0] == "M":
                        hidden(n, k)
                    if job[0] == "G":
                        gated(n, k)
                for k in range(KD):
                    if slot == SLOT[f"D{k}"] + 2:
                        softplus_sum(n, k)

            def main(c):
                n = c + 1
                for slot in range(STATES):
                    d, s = at_state(c, slot, SCAN)
                    if d.real:
                        scan(d, s)
                        if (s + 1) % H_RING == 0 and (d + 1).real:
                            keep_carry(d, s)
                    d, s = at_state(c, slot, BX)
                    if d.real and s in DVE_B:
                        bx(d, s)
                    if c.real:
                        front(c, slot + STATES)
                    if n.real:
                        front(n, slot)
                    if slot == FINISH_Y and (c + -1).real:
                        finish_y(c + -1)
                    for t in range(NT):
                        if slot == SLOT[f"O{t}"] + 1 and (c + -1).real:
                            add_residual(c + -1, t)

            V.memset(bias_x3[PARTS * BC:SPREAD, :], 0.0).then_inc(s_nobias, 1)
            V.memset(carry[:], 0.0).then_inc(s_carry, 1)
            whole_run(dve, main, steps, DVE_STEPS)

        @block.tensor
        def _(pe):
            mm = nc.tensor.matmul

            def bank_for(n, job):
                found = job_before(n, job)
                if found:
                    m, before = found
                    kind, j = before[0], int(before[1])
                    if kind == "T":
                        pe.wait_ge(s_xnT, m.count(1, 1))
                    elif kind == "R":
                        pe.wait_ge(s_logits, m.count(1, 1))
                    elif kind == "Z":
                        pe.wait_ge(s_xz, m.count(2 * KD, j + 1))
                    elif kind == "A":
                        pe.wait_ge(s_up, m.count(ET, j + 1))
                    elif kind == "O":
                        pe.wait_ge(s_out, m.count(NT, j + 1 - 2 * NT))
                    elif kind == "X":
                        pe.wait_ge(s_xdbl, m.count(1, 1))
                    elif kind == "D":
                        pe.wait_ge(s_relu, m.count(KD, j + 1))
                    elif kind == "M":
                        pe.wait_ge(s_hid, m.count(ET, j + 1))
                    elif kind == "G":
                        pe.wait_ge(s_gated, m.count(RT, j + 1))
                return job_ps[BANK[job]]

            def project_out(c, t, ps):
                if t == 0:
                    pe.wait_ge(s_gated, c.count(RT, RT))
                    pe.wait_ge(s_hid, c.count(ET, ET))
                    pe.wait_ge(s_yz, c.count(1, 1))
                tile = slice(t * P, (t + 1) * P)
                for j in range(ET):
                    mm(ps[:, 0:D], hid[:, c.parity, j, tile], w2[:, j], start=(j == 0), stop=False)
                for k in range(KD):
                    ins = mm(ps[:, 0:D], yz[:, k, tile], w_out[:, k], start=False, stop=(k == KD - 1))
                ins.then_inc(s_O, 1)

            def front_job(n, job):
                ps = bank_for(n, job)
                u = xz[:, n.parity]
                kind, j = job[0], int(job[1])
                if kind == "T" and n.first:
                    pe.wait_ge(s_ident, 16)
                if kind == "R" and n.first:
                    pe.wait_ge(s_first, 16 * N_FIRST)
                if kind == "X" and n.first:
                    pe.wait_ge(s_small, 16 * N_SMALL)
                if kind == "D" and n.first:
                    pe.wait_ge(s_weights, 16 * N_WEIGHTS)
                if kind == "G" and n.first:
                    pe.wait_ge(s_selector, 2)
                if kind == "T":
                    pe.wait_ge(s_xn, n.count(1, 1))
                    for t in range(NT):
                        ins = nc.tensor.transpose(ps[:, t * P:(t + 1) * P], xn[:, t], ident[:])
                    ins.then_inc(s_T, 1)
                if kind == "R":
                    pe.wait_ge(s_xnT, n.count(1, 1))
                    for t in range(NT):
                        ins = mm(ps[:, t * EXPERTS:(t + 1) * EXPERTS], xn_t[:, t * P:(t + 1) * P], w_r[:],
                                 start=True, stop=True)
                    ins.then_inc(s_R, 1)
                if kind == "Z":
                    mm(ps[:], w_in[:, j * P:(j + 1) * P], xn_t[:], start=True, stop=True).then_inc(s_Z, 1)
                if kind == "A":
                    mm(ps[:], w1[:, EPT * j:EPT * (j + 1)], xn_t[:], start=True, stop=True).then_inc(s_A, 1)
                if kind == "O":
                    project_out(n + -2, j, ps)
                if kind == "X":
                    pe.wait_ge(s_gates, n.count(1, 1))
                    for k in range(KD):
                        mm(ps[0:PARTS * BC, :], w_x3[:, k], u[:, k], start=(k == 0), stop=(k == KD - 1))
                    for t in range(NT):
                        ins = mm(ps[PARTS * BC:SPREAD, t * P:(t + 1) * P],
                                 gates3[:, t].rearrange("p q e -> p (q e)"), ident[:], start=True, stop=True)
                    ins.then_inc(s_X, 1)
                if kind == "D":
                    if j == 0:
                        pe.wait_ge(s_silu, n.count(1, 1))
                    for k in range(KD):
                        ins = mm(ps[:], w_dt[:, k, j * P:(j + 1) * P], u[:, k], start=(k == 0), stop=(k == KD - 1))
                    ins.then_inc(s_D, 1)
                if kind == "M":
                    mm(ps[:], w3[:, EPT * j:EPT * (j + 1)], xn_t[:], start=True, stop=True).then_inc(s_M, 1)
                if kind == "G":
                    pe.wait_ge(s_parts, n.count(1, 1))
                    mm(ps[:], selector[:, ND + j], parts[:, n.parity], start=True, stop=True).then_inc(s_Gps, 1)

            def spread_b(c, s):
                k = DVE_B.index(s)
                if k == 0:
                    pe.wait_ge(s_parts, c.count(1, 1))
                if k > 0 or c.since(1):
                    pe.wait_ge(s_bxd, c.count(len(DVE_B), k))
                mm(b_ps[:], selector[:, k], parts[:, c.parity], start=True, stop=True).then_inc(s_Bps, 1)

            def sum_states(c, s):
                pe.wait_ge(s_hc, c.count(STATES, s + 1))
                if s == 0 and c.since(1):
                    pe.wait_ge(s_yz, c.count(1, 0))
                for d in range(KD):
                    ins = mm(y_ps[:, d], ident[:], hc[:, s % Y_RING, d], start=(s == 0), stop=(s == STATES - 1))
                ins.then_inc(s_sum, 1)

            def jobs(n, slot):
                for job in JOBS:
                    if SLOT.get(job) == slot and job_lives(n, job):
                        front_job(n, job)

            def main(c):
                for slot in range(STATES):
                    d, s = at_state(c, slot, SUM)
                    if d.real and s > 0:
                        sum_states(d, s)
                    e, i = at_state(c, slot, SPREAD_B)
                    if e.real and i in DVE_B:
                        spread_b(e, i)
                    jobs(c, slot + STATES)
                    jobs(c + 1, slot)
                    if d.real and s == 0:
                        sum_states(d, s)

            whole_run(pe, main, first=2, last=CHUNKS - 3)


_INS = ["L0_attn_x", "L0_attn_W_in", "L0_attn_b_in", "L0_attn_W_x", "L0_attn_b_x", "L0_attn_W_dt", "L0_attn_b_dt",
        "L0_attn_W_out", "L0_attn_b_out", "L0_attn_A_log", "L0_attn_D_param", "L0_ffn_router_w", "L0_ffn_router_b",
        "L0_ffn_routed_w1", "L0_ffn_routed_w3", "L0_ffn_routed_w2", "L0_ffn_shared_w1", "L0_ffn_shared_w3",
        "L0_ffn_shared_w2"]


def _constants(np):
    rows = np.zeros((SPREAD, ND + EXPERTS), np.float32)
    mask = np.zeros((SPREAD, 2), np.float32)
    for q in range(PARTS):
        for k, s in enumerate(DVE_B):
            rows[q * BC + s, k] = 1
        for e in range(EXPERTS):
            rows[PARTS * BC + q * EXPERTS + e, ND + e] = 1
        for r in (slice(q * BC, (q + 1) * BC), slice(PARTS * BC + q * EXPERTS, PARTS * BC + (q + 1) * EXPERTS)):
            mask[r, 0] = -1.0 if q >= 1 else 0.0
            mask[r, 1] = -1.0 if q >= 2 else 0.0
    keep = np.zeros((P, 2, CHUNKS), np.float32)
    for c in range(CHUNKS):
        if c % CPB:
            keep[:, 0, c], keep[:, 1, c] = -BIG, BIG
    iota = np.tile(np.arange(EXPERTS, dtype=np.float32), (P, 1))
    return [("ident", np.eye(P, dtype=np.float32)), ("rows", rows), ("part_mask", mask), ("iota", iota),
            ("keep", keep)]


def kernel(**inputs):
    import numpy as _np
    import concourse.bacc as _bacc
    from concourse.bass_utils import run_bass_kernel_spmd as _run

    nc = _bacc.Bacc("TRN2", target_bir_lowering=False, num_devices=1)
    arrays, args = {}, []
    data = {n: _np.asarray(inputs[n]) for n in _INS}
    for n in ("L0_attn_b_in", "L0_attn_b_dt", "L0_attn_D_param"):
        data[n] = data[n].reshape(-1, P).T
    for name, a in list(data.items()) + _constants(_np):
        a = _np.ascontiguousarray(a)
        arrays[f"in_{name}_dram"] = a
        args.append(nc.dram_tensor(f"in_{name}_dram", a.shape, mybir.dt.from_np(a.dtype), kind="ExternalInput").ap())
    args.append(nc.dram_tensor("bc_rows", (2, BC, CHUNK), F32, kind="Internal").ap())
    args.append(nc.dram_tensor("out_dram", (BATCH, SEQ, D), F32, kind="ExternalOutput").ap())
    mixed_layer_program(nc, *args)
    r = _run(nc, [arrays], core_ids=[0])
    return r.results[0]["out_dram"]
```

```python
import concourse.bass as bass
from concourse import mybir
from contextlib import ExitStack

F32 = mybir.dt.float32
BF16 = mybir.dt.bfloat16
U32 = mybir.dt.uint32
ALU = mybir.AluOpType
ACT = mybir.ActivationFunctionType
EXP_LN_SET = "natural_log_exp_and_others"

P = 128
BATCH, SEQ, D = 2, 2048, 128
INNER, STATES = 256, 16
KD = INNER // P
EXPERTS, SHARED, H = 8, 2, 64
EPT = P // H
RT = EXPERTS // EPT
ET = (EXPERTS + SHARED) // EPT
CHUNK = 512
NT = CHUNK // P
CHUNKS = BATCH * SEQ // CHUNK
CPB = SEQ // CHUNK
PARTS = 3
BC = 2 * STATES
SPREAD = PARTS * (BC + EXPERTS)
EPS = 1e-5
BIG = 3.4028234e38

POOL_B = [1, 3, 5, 7, 10, 12, 14]
DVE_B = [s for s in range(STATES) if s not in POOL_B]
POOL_B_LAST = [1, 5, 9, 13]
DVE_C_LAST = [STATES - 3, STATES - 1]
C_RING, Y_RING, B_RING, BX_DVE_RING, BX_POOL_RING, H_RING = 4, 8, 2, 3, 2, 8
assert 2 * len(POOL_B) % BX_POOL_RING == 0 and 2 * len(DVE_B) % BX_DVE_RING == 0
assert 2 * len(POOL_B) % B_RING == 0
N_FIRST, N_WEIGHTS, N_SMALL = 3, 13 + PARTS, 4
ACT_STEPS, DVE_STEPS = 2 * 4, 2 * 2

SLOT = {"T0": 6, "R0": 7, "Z0": 8, "Z1": 8, "Z2": 9, "Z3": 9, "O0": 10, "A0": 10, "X0": 11, "D0": 12, "D1": 13,
        "O1": 15, "O2": 16, "O3": 16, "A1": 17, "A2": 17, "A3": 18, "A4": 18, "M0": 19, "M1": 19,
        "G0": 20, "M2": 20, "G1": 21, "G2": 21, "M3": 21, "G3": 22, "M4": 22}
JOBS = list(SLOT)
JOB_BANKS = 3
JOBS[1:1] = ["--", "--"]
JOBS.insert(JOBS.index("D1") + 1, "--")
assert len(JOBS) % JOB_BANKS == 0
SLOT_LAST = {"O0": 10, "O1": 11, "O2": 12, "O3": 13}
EXPERTS_LAST = [14, 15, 16, 20]
BANK = {job: i % JOB_BANKS for i, job in enumerate(JOBS)}
LOAD_B, SPREAD_B, BX, DECAY, SCAN, LOAD_C, TIMES_C, SUM = 0, 0, -1, -3, -4, -4, -5, -8
STATS, RSTD, NORM, FINISH_Y, TOP2, DIFF, RATIO, TOTAL, GATES, SILU_XZ = 2, 2, 4, 7, 8, 8, 9, 10, 10, 10
SAVE_BC, REST_1, PART_2, REST_2, DTU, SILU_UP = 13, 13, 14, 15, (14, 15), 19
LOAD_X, LOAD_RESIDUAL, SEND = 8, 7, 5


def slot_of(n, job):
    if n.turn is None and n.k == CHUNKS and job in SLOT_LAST:
        return SLOT_LAST[job]
    return SLOT.get(job)


class Chunk:

    def __init__(self, k, turn=None):
        self.k, self.turn, self.parity = k, turn, k % 2

    def __add__(self, d):
        return Chunk(self.k + d, self.turn)

    def count(self, per, more):
        v = per * self.k + more
        return v if self.turn is None else self.turn * (2 * per) + v

    @property
    def index(self):
        return self.count(1, 0)

    def since(self, k):
        return self.turn is not None or self.k >= k

    @property
    def last(self):
        return self.turn is None and self.k == CHUNKS - 1

    @property
    def pool_b(self):
        return POOL_B_LAST if self.last else POOL_B

    @property
    def dve_b(self):
        return [s for s in range(STATES) if s not in self.pool_b]

    @property
    def dve_c(self):
        return DVE_C_LAST if self.last else []

    def pool_c_before(self, s):
        return len([i for i in range(s) if i not in self.dve_c])

    @property
    def first(self):
        return self.turn is None and self.k == 0

    @property
    def real(self):
        return self.turn is not None or 0 <= self.k < CHUNKS


def ring_slot(c, per, k, ring):
    return (per * c.k + k) % ring


def ring_fills(c, per, k, ring):
    fills = (per * c.k + k) // ring + 1
    return fills if c.turn is None else c.turn * (2 * per // ring) + fills


class Steps:

    def __init__(self):
        self.n, self.turn, self.per = 0, None, 0

    def next(self):
        self.n += 1
        return self.n if self.turn is None else self.turn * self.per + self.n

    def enter(self, turn, per):
        self.turn, self.per, self.base = turn, per, self.n

    def leave(self, turns):
        assert self.n - self.base == self.per, (self.n - self.base, self.per)
        self.n, self.turn = self.base + turns * self.per, None


def job_before(n, job):
    i = JOBS.index(job) - JOB_BANKS
    while True:
        m = n if i >= 0 else n + -1
        before = JOBS[i % len(JOBS)]
        if before == "--" or not job_lives(m, before):
            i -= JOB_BANKS
            if m.turn is None and m.k < 0:
                return None
            if i < -len(JOBS):
                return None
            continue
        return m, before


def job_lives(n, job):
    return n.turn is not None or (0 <= n.k - 2 < CHUNKS - 1 if job[0] == "O" else n.real)


def at_state(c, slot, ahead):
    return c + (slot + ahead) // STATES, (slot + ahead) % STATES


def mixed_layer_program(nc, x, W_in, b_in, W_x, b_x, W_dt, b_dt, W_out, b_out, A_log, D_param,
                        router_w, router_b, routed_w1, routed_w3, routed_w2,
                        shared_w1, shared_w3, shared_w2, ident_c, rows_c, part_mask_c, iota_c, keep_c, bc_rows, out):
    x_v = x.rearrange("b s d -> (b s) d").rearrange("(c n p) d -> c p n d", n=NT, p=P)
    out_v = out.rearrange("b s d -> (b s) d").rearrange("(c n p) d -> c p n d", n=NT, p=P)
    ctx = ExitStack()
    with ctx:
        def sb(name, shape, dt=F32):
            return ctx.enter_context(nc.sbuf_tensor(name, shape, dt))

        def pb(name, shape):
            return ctx.enter_context(nc.psum_tensor(name, shape, F32))

        def sem(name):
            return ctx.enter_context(nc.semaphore(name))

        w_in = sb("w_in", [P, 2 * INNER])
        w_x3 = sb("w_x3", [P, KD, PARTS * BC])
        w_dt = sb("w_dt", [P, KD, INNER])
        w_out = sb("w_out", [P, KD, D])
        w_r = sb("w_r", [P, EXPERTS])
        w1 = sb("w1", [P, EXPERTS + SHARED, H])
        w3 = sb("w3", [P, EXPERTS + SHARED, H])
        w2 = sb("w2", [P, ET, D])
        bias_in = sb("bias_in", [P, 2 * KD])
        bias_x3 = sb("bias_x3", [SPREAD, 1])
        bias_dt = sb("bias_dt", [P, KD])
        bias_out = sb("bias_out", [1, D])
        ones = sb("ones", [1, P])
        bias_r = sb("bias_r", [P, EXPERTS])
        d_par = sb("d_par", [P, KD])
        a_log = sb("a_log", [P, KD, STATES])
        a_neg = sb("a_neg", [P, KD, STATES])
        ident = sb("ident", [P, P])
        selector = sb("selector", [SPREAD, STATES + RT, P], BF16)
        rows = sb("rows", [SPREAD, STATES + EXPERTS])
        part_mask = sb("part_mask", [SPREAD, 2])
        iota = sb("iota", [P, EXPERTS])
        keep = sb("keep", [P, 2, CHUNKS])
        minus_half = sb("minus_half", [P, NT])
        minus_one = sb("minus_one", [P, NT])
        eps = sb("eps", [P, NT])
        seat = sb("seat", [P, 1])

        x_t = sb("x_t", [P, 2, NT, D])
        x_res = sb("x_res", [P, NT, D])
        stats = sb("stats", [P, NT, 6])
        mean_var = sb("mean_var", [P, NT, 2])
        var_eps = sb("var_eps", [P, NT])
        rstd = sb("rstd", [P, NT])
        minus_mean = sb("minus_mean", [P, NT])
        shift = sb("shift", [P, NT])
        xn = sb("xn", [P, NT, D])
        xn_t = sb("xn_t", [P, CHUNK])
        logits = sb("logits", [P, NT, EXPERTS])
        top = sb("top", [P, NT, 8])
        top_at = sb("top_at", [P, NT, 8], U32)
        top_f = sb("top_f", [P, NT, 2])
        diff = sb("diff", [P, NT])
        ratio = sb("ratio", [P, NT])
        total = sb("total", [P, NT])
        gate = sb("gate", [P, NT, 2])
        pick = sb("pick", [P, NT, 2, EXPERTS])
        gates3 = sb("gates3", [P, NT, PARTS, EXPERTS])

        xz = sb("xz", [P, 2, 2 * KD, CHUNK])
        up = sb("up", [P, ET, CHUNK])
        hid = sb("hid", [P, 2, ET, CHUNK])
        bc_sb = sb("bc_sb", [BC, CHUNK])
        part = sb("part", [SPREAD, CHUNK], BF16)
        parts = sb("parts", [SPREAD, 2, CHUNK], BF16)
        soft = sb("soft", [P, KD, CHUNK])
        dt = sb("dt", [P, 2, KD, CHUNK])
        dtu = sb("dtu", [P, 2, KD, CHUNK])
        yz = sb("yz", [P, KD, CHUNK])
        out_sb = sb("out_sb", [P, NT, D])

        carry = sb("carry", [P, KD, STATES])
        h_ring = sb("h_ring", [P, KD, H_RING, CHUNK])
        bx_dve = sb("bx_dve", [P, BX_DVE_RING, KD, CHUNK])
        bx_pool = sb("bx_pool", [P, BX_POOL_RING, KD, CHUNK])
        b_sb = sb("b_sb", [P, B_RING, CHUNK])
        c_sb = sb("c_sb", [P, C_RING, CHUNK])
        hc = sb("hc", [P, Y_RING, KD, CHUNK])

        y_ps = pb("y_ps", [P, KD, CHUNK])
        decay_ps = pb("decay_ps", [P, KD, CHUNK])
        b_ps = pb("b_ps", [P, CHUNK])
        job_ps = [pb(f"job_ps{i}", [P, CHUNK]) for i in range(JOB_BANKS)]
        last_ps = job_ps + [b_ps]
        assert len(last_ps) == NT

        s_ident = sem("identity_loaded")
        s_first = sem("first_loads")
        s_weights = sem("weights_loaded")
        s_small = sem("small_loaded")
        s_selector = sem("selector_made")
        s_x = [sem("x_even_loaded"), sem("x_odd_loaded")]
        s_res = sem("residual_loaded")
        s_half = sem("minus_half_set")
        s_biasx = sem("bias_x_loaded")
        s_nobias = sem("gates_bias_zeroed")
        s_a = sem("a_ready")
        s_stats = sem("stats_ready")
        s_vareps = sem("var_eps_ready")
        s_rstd = sem("rstd_ready")
        s_shift = sem("shift_ready")
        s_xn = sem("xn_ready")
        s_T = sem("transposed")
        s_xnT = sem("xn_t_ready")
        s_R = sem("logits_done")
        s_logits = sem("logits_read")
        s_diff = sem("diff_ready")
        s_top = sem("top_two_found")
        s_ratio = sem("ratio_ready")
        s_total = sem("total_ready")
        s_gate1 = sem("gate_1_ready")
        s_gate2 = sem("gate_2_ready")
        s_pick = sem("picks_weighted")
        s_gates = sem("gates_ready")
        s_Z = sem("in_proj_done")
        s_xz = sem("in_proj_read")
        s_A = sem("w1_done")
        s_up = sem("w1_read")
        s_silu = sem("silu_done")
        s_upsilu = sem("up_silu_done")
        s_X = sem("x_dbl_done")
        s_biased = sem("x_dbl_biased")
        s_xdbl = sem("bc_copied")
        s_p1 = sem("part1_ready")
        s_r1 = sem("rest1_ready")
        s_p2 = sem("part2_ready")
        s_parts = sem("parts_ready")
        s_D = sem("dt_proj_done")
        s_soft = sem("softplus_ready")
        s_dt = sem("dt_ready")
        s_dtu = sem("dtu_ready")
        s_M = sem("w3_done")
        s_hid = sem("hid_ungated")
        s_gated = sem("hid_gated")
        s_Bps = sem("b_spread")
        s_Gps = sem("gate_spread")
        s_saved = sem("bc_saved")
        s_Bsb = [sem(f"b_loaded_{i}") for i in range(B_RING)]
        s_Csb = [sem(f"c_loaded_{i}") for i in range(C_RING)]
        s_bxd = sem("bx_by_dve")
        s_bxp = sem("bx_by_pool")
        s_decay = sem("decay_ready")
        s_scan = sem("scanned")
        s_carry = sem("carry_ready")
        s_hc = sem("hc_ready")
        s_hc_dve = sem("hc_by_dve")
        s_sum = sem("summed")
        s_skip = sem("skip_added")
        s_yz = sem("yz_ready")
        s_O = sem("out_proj_done")
        s_out = sem("out_added")
        s_sent = sem("out_sent")
        s_dve = sem("dve_step")
        s_act = sem("act_step")

        block = ctx.enter_context(nc.Block())

        def whole_run(eng, main, steps=None, per=0, first=1, last=CHUNKS - 2):
            chunks = [Chunk(k) for k in range(-1, CHUNKS + 1)]
            pairs = (last - first + 1) // 2
            for c in chunks[:first + 1]:
                main(c)
            with eng.Fori(0, pairs) as turn:
                if steps:
                    steps.enter(turn, per)
                main(Chunk(first, turn))
                main(Chunk(first + 1, turn))
                if steps:
                    steps.leave(pairs)
            for c in chunks[last + 2:]:
                main(c)

        @block.sync
        def _(sp):
            def load_x(c):
                if c.since(2):
                    sp.wait_ge(s_xn, c.count(1, -1))
                sp.dma_start(x_t[:, c.parity], x_v[c.index]).then_inc(s_x[c.parity], 16)

            def load_residual(c):
                if c.since(1):
                    sp.wait_ge(s_sent, c.count(16, 0))
                sp.dma_start(x_res[:], x_v[c.index]).then_inc(s_res, 16)

            def send(c):
                sp.wait_ge(s_out, c.count(NT, NT))
                sp.dma_start(out_v[c.index], out_sb[:]).then_inc(s_sent, 16)

            def save_bc(n):
                sp.wait_ge(s_xdbl, n.count(1, 1))
                sp.dma_start(bc_rows[n.parity], bc_sb[:]).then_inc(s_saved, 16)

            def load_b(c, s):
                k = c.pool_b.index(s)
                if k == 0 and c.turn is None:
                    sp.wait_ge(s_saved, c.count(16, 16))
                if k >= B_RING or c.since(1):
                    sp.wait_ge(s_bxp, c.count(len(POOL_B), k + 1 - B_RING))
                i = ring_slot(c, len(POOL_B), k, B_RING)
                sp.dma_start(b_sb[:, i], bc_rows[c.parity, s:s + 1, :].to_broadcast([P, CHUNK])
                             ).then_inc(s_Bsb[i], 16)

            def load_c(c, s):
                if s >= C_RING or c.since(1):
                    sp.wait_ge(s_hc, c.count(STATES, s + 1 - C_RING))
                sp.dma_start(c_sb[:, s % C_RING],
                             bc_rows[c.parity, STATES + s:STATES + s + 1, :].to_broadcast([P, CHUNK])
                             ).then_inc(s_Csb[s % C_RING], 16)

            def main(c):
                n = c + 1
                for slot in range(STATES):
                    d, s = at_state(c, slot, LOAD_C)
                    if d.real:
                        load_c(d, s)
                    d, s = at_state(c, slot, LOAD_B)
                    if d.real and s in d.pool_b:
                        load_b(d, s)
                    if slot == SEND and (c + -2).real:
                        send(c + -2)
                    if slot == SAVE_BC and n.real:
                        save_bc(n)
                    if slot == LOAD_X and (n + 1).real and (n + 1).since(2):
                        load_x(n + 1)
                    if slot == LOAD_RESIDUAL and (c + -1).real:
                        load_residual(c + -1)

            load_x(Chunk(0))
            sp.dma_start(ident[:], ident_c).then_inc(s_ident, 16)
            for dst, src in [
                (w_r[:], router_w), (w_in[:], W_in), (iota[:], iota_c),
            ]:
                sp.dma_start(dst, src).then_inc(s_first, 16)
            for dst, src in [
                (w1[:, 0:EXPERTS, :], routed_w1.rearrange("e d h -> d e h")),
                (w1[:, EXPERTS:, :], shared_w1.rearrange("e d h -> d e h")),
                *[(w_x3[:, :, q * BC:(q + 1) * BC], W_x.rearrange("(k p) n -> p k n", p=P)) for q in range(PARTS)],
                (rows[:], rows_c), (part_mask[:], part_mask_c),
                (w_dt[:], W_dt.rearrange("(k p) n -> p k n", p=P)),
                (w3[:, 0:EXPERTS, :], routed_w3.rearrange("e d h -> d e h")),
                (w3[:, EXPERTS:, :], shared_w3.rearrange("e d h -> d e h")),
                (keep[:], keep_c), (d_par[:], D_param),
                (bias_out[:], b_out.rearrange("(a d) -> a d", a=1)),
                (w_out[:], W_out.rearrange("(k p) n -> p k n", p=P)),
                (w2[:, 0:RT, :], routed_w2.rearrange("(j e) h d -> (e h) j d", e=EPT)),
                (w2[:, RT, :], shared_w2.rearrange("e h d -> (e h) d")),
            ]:
                sp.dma_start(dst, src).then_inc(s_weights, 16)
            load_x(Chunk(1))
            whole_run(sp, main, first=2, last=CHUNKS - 3)
            send(Chunk(CHUNKS - 1))
            sp.wait_ge(s_sent, 16 * CHUNKS)
            sp.wait_ge(s_saved, 16 * CHUNKS)

        @block.gpsimd
        def _(pool):
            def inverse_deviation(n):
                pool.wait_ge(s_stats, n.count(1, 1))
                pool.tensor_tensor(minus_mean[:], mean_var[:, :, 0], minus_one[:], ALU.mult)
                pool.tensor_tensor(var_eps[:], mean_var[:, :, 1], eps[:], ALU.add).then_inc(s_vareps, 1)
                pool.wait_ge(s_vareps, n.count(1, 1))
                pool.tensor_tensor(rstd[:], var_eps[:], minus_half[:], ALU.pow).then_inc(s_rstd, 1)
                pool.wait_ge(s_rstd, n.count(1, 1))
                pool.tensor_tensor(shift[:], minus_mean[:], rstd[:], ALU.mult).then_inc(s_shift, 1)

            def wide(ap):
                return ap.unsqueeze(3).to_broadcast([P, NT, 2, EXPERTS])

            def second_less_first(n):
                pool.wait_ge(s_top, n.count(1, 1))
                pool.tensor_tensor(diff[:], top[:, :, 1], top[:, :, 0], ALU.subtract).then_inc(s_diff, 1)
                pool.tensor_copy(top_f[:], top_at[:, :, 0:2]).then_inc(s_diff, 1)

            def gates(n):
                pool.wait_ge(s_gate1, n.count(1, 1))
                pool.tensor_tensor(gate[:, :, 1], ratio[:], gate[:, :, 0], ALU.mult).then_inc(s_gate2, 1)
                pool.wait_ge(s_gate2, n.count(1, 1))
                pool.tensor_tensor(pick[:], pick[:], wide(gate[:]), ALU.mult).then_inc(s_pick, 1)
                pool.wait_ge(s_pick, n.count(1, 1))
                for q in range(PARTS):
                    ins = pool.tensor_tensor(gates3[:, :, q], pick[:, :, 0], pick[:, :, 1], ALU.add)
                ins.then_inc(s_gates, 1)

            def make_selectors():
                pool.wait_ge(s_weights, 16 * N_WEIGHTS)
                pool.tensor_copy(selector[:, 0:STATES], rows[:, 0:STATES].unsqueeze(2).to_broadcast([SPREAD, STATES, P])
                                 ).then_inc(s_selector, 1)
                pool.tensor_copy(selector[:, STATES:].rearrange("r j (e h) -> r (j e) h", e=EPT),
                                 rows[:, STATES:].unsqueeze(2).to_broadcast([SPREAD, EXPERTS, H])).then_inc(s_selector, 1)

            def dt_times_u(n, k):
                pool.wait_ge(s_dt, n.count(KD, k + 1))
                pool.tensor_tensor(dtu[:, n.parity, k], dt[:, n.parity, k], xz[:, n.parity, k],
                                   ALU.mult).then_inc(s_dtu, 1)

            def bx(c, s):
                k = c.pool_b.index(s)
                if k == 0:
                    pool.wait_ge(s_dtu, c.count(KD, KD))
                i, loads = ring_slot(c, len(POOL_B), k, B_RING), ring_fills(c, len(POOL_B), k, B_RING)
                pool.wait_ge(s_Bsb[i], loads * 16)
                before = (c.pool_b if k >= BX_POOL_RING else POOL_B)[k - BX_POOL_RING]
                if k >= BX_POOL_RING:
                    pool.wait_ge(s_scan, c.count(KD * STATES, KD * (before + 1)))
                elif c.since(1):
                    pool.wait_ge(s_scan, c.count(KD * STATES, KD * (before + 1 - STATES)))
                pool.tensor_tensor(bx_pool[:, ring_slot(c, len(POOL_B), k, BX_POOL_RING)], dtu[:, c.parity],
                                   b_sb[:, i].unsqueeze(1).to_broadcast([P, KD, CHUNK]),
                                   ALU.mult).then_inc(s_bxp, 1)

            def h_times_c(c, s):
                loads = STATES // C_RING
                pool.wait_ge(s_Csb[s % C_RING], c.count(16 * loads, 16 * (s // C_RING + 1)))
                pool.wait_ge(s_scan, c.count(KD * STATES, KD * (s + 1)))
                if s >= Y_RING or c.since(1):
                    pool.wait_ge(s_sum, c.count(STATES, s + 1 - Y_RING))
                pool.tensor_tensor(hc[:, s % Y_RING], h_ring[:, :, s % H_RING],
                                   c_sb[:, s % C_RING].unsqueeze(1).to_broadcast([P, KD, CHUNK]),
                                   ALU.mult).then_inc(s_hc, 1)

            def main(c):
                for slot in range(STATES):
                    n = c + 1
                    d, s = at_state(c, slot, BX)
                    if d.real and s in d.pool_b:
                        bx(d, s)
                    if slot == RSTD and n.real:
                        inverse_deviation(n)
                    if slot == DIFF and n.real:
                        second_less_first(n)
                    if slot == GATES and n.real:
                        gates(n)
                        if n.first:
                            make_selectors()
                    if slot in DTU and n.real:
                        dt_times_u(n, DTU.index(slot))
                    d, s = at_state(c, slot, TIMES_C)
                    if d.real and s not in d.dve_c:
                        h_times_c(d, s)

            for q in range(PARTS):
                pool.dma_start(bias_x3[q * BC:(q + 1) * BC, :], b_x.rearrange("(n a) -> n a", a=1)
                               ).then_inc(s_biasx, 16)
            pool.memset(minus_half[:], -0.5).then_inc(s_half, 1)
            pool.memset(eps[:], EPS).then_inc(s_half, 1)
            pool.memset(minus_one[:], -1.0).then_inc(s_half, 1)
            pool.wait_ge(s_half, 3)
            whole_run(pool, main)

        @block.scalar
        def _(act):
            steps = Steps()

            def normalise(n):
                act.wait_ge(s_shift, n.count(1, 1))
                for t in range(NT):
                    ins = nc.scalar.activation(xn[:, t], x_t[:, n.parity, t], ACT.Identity,
                                               scale=rstd[:, t:t + 1], bias=shift[:, t:t + 1])
                ins.then_inc(s_xn, 1)

            def transposed_rows(n):
                act.wait_ge(s_T, n.count(1, 1))
                nc.scalar.copy(xn_t[:], job_ps[BANK["T0"]][:]).then_inc(s_xnT, 1)

            def decay_rates():
                act.wait_ge(s_small, 16 * N_SMALL)
                nc.scalar.activation(a_neg[:], a_log[:], ACT.Exp).then_inc(s_a, 1)
                act.wait_ge(s_a, 1)
                nc.scalar.activation(a_neg[:], a_neg[:], ACT.Copy, scale=-1.0).then_inc(s_a, 1)

            def input_projection(n, m):
                if m == 0 and n.since(2):
                    act.wait_ge(s_yz, n.count(1, -1))
                if m == 0 and n.first:
                    decay_rates()
                act.wait_ge(s_Z, n.count(2 * KD, m + 1))
                nc.scalar.activation(xz[:, n.parity, m], job_ps[BANK[f"Z{m}"]][:], ACT.Identity,
                                     bias=bias_in[:, m:m + 1]).then_inc(s_xz, 1)

            def expert_up(n, j):
                act.wait_ge(s_A, n.count(ET, j + 1))
                nc.scalar.copy(up[:, j], job_ps[BANK[f"A{j}"]][:]).then_inc(s_up, 1)

            def first_part(n):
                ps = job_ps[BANK["X0"]][0:SPREAD, :]
                if n.first:
                    act.wait_ge(s_biasx, 16 * PARTS)
                    act.wait_ge(s_nobias, 1)
                act.wait_ge(s_X, n.count(1, 1))
                nc.scalar.activation(ps, ps, ACT.Identity, bias=bias_x3[:, 0:1]).then_inc(s_biased, 1)
                act.wait_ge(s_biased, n.count(1, 1))
                nc.scalar.copy(bc_sb[:], ps[0:BC, :]).then_inc(s_xdbl, 1)
                nc.scalar.copy(part[:], ps).then_inc(s_p1, 1)

            def second_part(n):
                act.wait_ge(s_r1, n.count(1, 1))
                nc.scalar.copy(part[:], job_ps[BANK["X0"]][0:SPREAD, :]).then_inc(s_p2, 1)

            def softplus_begin(n, k):
                ps = job_ps[BANK[f"D{k}"]]
                act.wait_ge(s_D, n.count(KD, k + 1))
                nc.scalar.activation(soft[:, k], ps[:], ACT.Abs, bias=bias_dt[:, k:k + 1]).then_inc(s_act, 1)
                nc.scalar.activation(ps[:], ps[:], ACT.Relu, bias=bias_dt[:, k:k + 1])

            def softplus_end(n, k):
                act.wait_ge(s_act, steps.next())
                nc.scalar.activation(soft[:, k], soft[:, k], ACT.Exp, scale=-1.0).then_inc(s_act, 1)
                act.wait_ge(s_act, steps.next())
                nc.scalar.activation(soft[:, k], soft[:, k], ACT.Ln, bias=1.0).then_inc(s_soft, 1)

            def silu_xz(n):
                act.wait_ge(s_xz, n.count(2 * KD, 2 * KD))
                u, z = xz[:, n.parity, 0:KD], xz[:, n.parity, KD:]
                nc.scalar.activation(u, u, ACT.Silu).then_inc(s_silu, 1)
                nc.scalar.activation(z, z, ACT.Silu).then_inc(s_silu, 1)
                nc.scalar.preload_act_table_set(EXP_LN_SET)

            def silu_up(n):
                act.wait_ge(s_up, n.count(ET, ET))
                nc.scalar.activation(up[:], up[:], ACT.Silu).then_inc(s_upsilu, 1)
                nc.scalar.preload_act_table_set(EXP_LN_SET)

            def gate_ratio(n):
                act.wait_ge(s_diff, n.count(2, 2))
                nc.scalar.activation(ratio[:], diff[:], ACT.Exp).then_inc(s_ratio, 1)
                act.wait_ge(s_ratio, n.count(1, 1))
                nc.scalar.activation(total[:], ratio[:], ACT.Identity, bias=1.0).then_inc(s_total, 1)

            def decay(c, s):
                if s == 0 and c.first:
                    act.wait_ge(s_a, 2)
                for k in range(KD):
                    if s == 0:
                        act.wait_ge(s_dt, c.count(KD, k + 1))
                    if s > 0 or c.since(1):
                        act.wait_ge(s_scan, c.count(KD * STATES, KD * (s - 1) + k + 1))
                    nc.scalar.activation(decay_ps[:, k], dt[:, c.parity, k], ACT.Exp,
                                         scale=a_neg[:, k, s:s + 1]).then_inc(s_decay, 1)

            def evacuate(n, slot):
                for job in JOBS:
                    k = int(job[1]) if job in SLOT else None
                    if SLOT.get(job) != slot - 1:
                        continue
                    if job[0] == "T":
                        transposed_rows(n)
                    if job[0] == "Z":
                        input_projection(n, k)
                    if job[0] == "A":
                        expert_up(n, k)
                    if job[0] == "X":
                        first_part(n)
                    if job[0] == "D":
                        softplus_begin(n, k)
                        softplus_end(n, k)

            def main(c):
                n = c + 1
                for slot in range(STATES):
                    d, s = at_state(c, slot, DECAY)
                    if d.real:
                        decay(d, s)
                    if c.real:
                        evacuate(c, slot + STATES)
                        if slot + STATES == SILU_UP:
                            silu_up(c)
                    if n.real and slot == PART_2:
                        second_part(n)
                    if n.real:
                        evacuate(n, slot)
                        if slot == NORM:
                            normalise(n)
                        if slot == RATIO:
                            gate_ratio(n)
                        if slot == SILU_XZ:
                            silu_xz(n)

            small = [
                (bias_in[:], b_in),
                (bias_r[:], router_b.rearrange("(a d) -> a d", a=1).to_broadcast([P, EXPERTS])),
                (bias_dt[:], b_dt), (a_log[:], A_log.rearrange("(k p) s -> p k s", p=P)),
            ]
            assert len(small) == N_SMALL
            for dst, src in small:
                act.dma_start(dst, src).then_inc(s_small, 16)
            nc.scalar.preload_act_table_set(EXP_LN_SET)
            whole_run(act, main, steps, ACT_STEPS)

        @block.vector
        def _(dve):
            V = nc.vector
            steps = Steps()

            def every_tile(ap):
                return ap.unsqueeze(1).to_broadcast([P, NT, EXPERTS])

            def norm_stats(n):
                loaded = 16 * (n.k // 2 + 1)
                dve.wait_ge(s_x[n.parity], loaded if n.turn is None else n.turn * 16 + loaded)
                for t in range(NT):
                    ins = V.bn_stats(stats[:, t], x_t[:, n.parity, t])
                ins.then_inc(s_dve, 1)
                dve.wait_ge(s_dve, steps.next())
                V.memset(seat[:], 0.0)
                for t in range(NT):
                    ins = V.bn_aggr(mean_var[:, t], stats[:, t])
                ins.then_inc(s_stats, 1)

            def route_top(n):
                if n.first:
                    dve.wait_ge(s_small, 16 * N_SMALL)
                    dve.wait_ge(s_first, 16 * N_FIRST)
                dve.wait_ge(s_R, n.count(1, 1))
                V.tensor_tensor(logits[:], job_ps[BANK["R0"]][:, 0:NT * EXPERTS].rearrange("p (t e) -> p t e", t=NT),
                                every_tile(bias_r[:]), ALU.add).then_inc(s_logits, 1)
                dve.wait_ge(s_logits, n.count(1, 1))
                V.memset(seat[:], 0.0)
                for t in range(NT):
                    ins = V.max(top[:, t], logits[:, t])
                ins.then_inc(s_dve, 1)
                dve.wait_ge(s_dve, steps.next())
                V.memset(seat[:], 0.0)
                for t in range(NT):
                    ins = V.max_index(top_at[:, t], top[:, t], logits[:, t])
                ins.then_inc(s_top, 1)

            def first_gate(n):
                dve.wait_ge(s_total, n.count(1, 1))
                V.tensor_tensor(pick[:], iota[:].unsqueeze(1).unsqueeze(1).to_broadcast([P, NT, 2, EXPERTS]),
                                top_f[:].unsqueeze(3).to_broadcast([P, NT, 2, EXPERTS]), ALU.is_equal)
                V.reciprocal(gate[:, :, 0], total[:]).then_inc(s_gate1, 1)

            def take_part_1(n):
                ps = job_ps[BANK["X0"]][0:SPREAD, :]
                if n.first:
                    dve.wait_ge(s_weights, 16 * N_WEIGHTS)
                dve.wait_ge(s_saved, n.count(16, 16))
                dve.wait_ge(s_p1, n.count(1, 1))
                V.scalar_tensor_tensor(ps, part[:], part_mask[:, 0:1], ps, ALU.mult, ALU.add).then_inc(s_r1, 1)

            def take_part_2(n):
                dve.wait_ge(s_p2, n.count(1, 1))
                V.scalar_tensor_tensor(parts[:, n.parity], part[:], part_mask[:, 1:2], job_ps[BANK["X0"]][0:SPREAD, :],
                                       ALU.mult, ALU.add).then_inc(s_parts, 1)

            def softplus_sum(n, k):
                dve.wait_ge(s_soft, n.count(KD, k + 1))
                V.tensor_tensor(dt[:, n.parity, k], job_ps[BANK[f"D{k}"]][:], soft[:, k], ALU.add).then_inc(s_dt, 1)

            def hidden(n, j):
                if j == 0:
                    dve.wait_ge(s_upsilu, n.count(1, 1))
                dve.wait_ge(s_M, n.count(ET, j + 1))
                V.tensor_tensor(hid[:, n.parity, j], job_ps[BANK[f"M{j}"]][:], up[:, j], ALU.mult).then_inc(s_hid, 1)

            def gated(n, j):
                dve.wait_ge(s_Gps, n.count(RT, j + 1))
                dve.wait_ge(s_hid, n.count(ET, j + 1))
                V.tensor_tensor(hid[:, n.parity, j], job_ps[BANK[f"G{j}"]][:], hid[:, n.parity, j],
                                ALU.mult).then_inc(s_gated, 1)

            def bx(c, s):
                k = c.dve_b.index(s)
                if k == 0:
                    dve.wait_ge(s_dtu, c.count(KD, KD))
                dve.wait_ge(s_Bps, c.count(len(DVE_B), k + 1))
                before = (c.dve_b if k >= BX_DVE_RING else DVE_B)[k - BX_DVE_RING]
                if k >= BX_DVE_RING:
                    dve.wait_ge(s_scan, c.count(KD * STATES, KD * (before + 1)))
                elif c.since(1):
                    dve.wait_ge(s_scan, c.count(KD * STATES, KD * (before + 1 - STATES)))
                V.tensor_tensor(bx_dve[:, ring_slot(c, len(DVE_B), k, BX_DVE_RING)], b_ps[:].unsqueeze(1).to_broadcast([P, KD, CHUNK]),
                                dtu[:, c.parity], ALU.mult).then_inc(s_bxd, 1)

            def scan(c, s):
                if s in c.pool_b:
                    k = c.pool_b.index(s)
                    bx_s = bx_pool[:, ring_slot(c, len(POOL_B), k, BX_POOL_RING)]
                    dve.wait_ge(s_bxp, c.count(len(POOL_B), k + 1))
                else:
                    k = c.dve_b.index(s)
                    bx_s = bx_dve[:, ring_slot(c, len(DVE_B), k, BX_DVE_RING)]
                    dve.wait_ge(s_bxd, c.count(len(DVE_B), k + 1))
                if s % H_RING == 0:
                    extra = 0 if c.turn is None and c.k == CHUNKS - 1 else s // H_RING
                    dve.wait_ge(s_carry, c.count(STATES // H_RING, 1 + extra))
                if s >= H_RING or c.since(1):
                    dve.wait_ge(s_hc, c.count(STATES, s + 1 - H_RING))
                for d in range(KD):
                    dve.wait_ge(s_decay, c.count(KD * STATES, KD * s + d + 1))
                    V.tensor_tensor_scan(h_ring[:, d, s % H_RING], decay_ps[:, d], bx_s[:, d],
                                         carry[:, d, s:s + 1], ALU.mult, ALU.add).then_inc(s_scan, 1)

            def keep_carry(c, s):
                dve.wait_ge(s_scan, c.count(KD * STATES, KD * (s + 1)))
                following = (c + 1).index
                V.tensor_scalar(carry[:, :, s + 1 - H_RING:s + 1], h_ring[:, :, :, CHUNK - 1],
                                keep[:, 0, bass.ds(following, 1)], keep[:, 1, bass.ds(following, 1)],
                                ALU.max, ALU.min).then_inc(s_carry, 1)

            def h_times_c(c, s):
                loads = STATES // C_RING
                dve.wait_ge(s_Csb[s % C_RING], c.count(16 * loads, 16 * (s // C_RING + 1)))
                dve.wait_ge(s_scan, c.count(KD * STATES, KD * (s + 1)))
                dve.wait_ge(s_sum, c.count(STATES, s + 1 - Y_RING))
                V.tensor_tensor(hc[:, s % Y_RING], h_ring[:, :, s % H_RING],
                                c_sb[:, s % C_RING].unsqueeze(1).to_broadcast([P, KD, CHUNK]),
                                ALU.mult).then_inc(s_hc_dve, 1)
                dve.wait_ge(s_hc_dve, 2 * c.dve_c.index(s) + 1)
                dve.wait_ge(s_hc, c.count(STATES, c.pool_c_before(s)))
                V.tensor_tensor(hc[:, s % Y_RING], hc[:, s % Y_RING], hc[:, (s - 1) % Y_RING],
                                ALU.add).then_inc(s_hc_dve, 1)

            def finish_y(c):
                dve.wait_ge(s_sum, c.count(STATES, STATES - len(c.dve_c)))
                for k in range(KD):
                    V.scalar_tensor_tensor(y_ps[:, k], xz[:, c.parity, k], d_par[:, k:k + 1], y_ps[:, k],
                                           ALU.mult, ALU.add).then_inc(s_skip, 1)
                dve.wait_ge(s_skip, c.count(KD, KD))
                V.tensor_tensor(yz[:], y_ps[:], xz[:, c.parity, KD:], ALU.mult).then_inc(s_yz, 1)

            def add_residual(c, t):
                dve.wait_ge(s_O, c.count(NT, t + 1))
                if t == 0:
                    dve.wait_ge(s_res, c.count(16, 16))
                ps = last_ps[t] if c.last else job_ps[BANK[f"O{t}"]]
                V.tensor_tensor(out_sb[:, t], ps[:, 0:D], x_res[:, t], ALU.add).then_inc(s_out, 1)

            def front(n, slot):
                if slot == STATS:
                    norm_stats(n)
                if slot == TOP2:
                    route_top(n)
                if slot == TOTAL:
                    first_gate(n)
                if slot == REST_1:
                    take_part_1(n)
                if slot == REST_2:
                    take_part_2(n)
                for job, k in [(job, int(job[1])) for job in JOBS if SLOT.get(job) == slot - 1]:
                    if job[0] == "M":
                        hidden(n, k)
                    if job[0] == "G":
                        gated(n, k)
                for k in range(KD):
                    if slot == SLOT[f"D{k}"] + 2:
                        softplus_sum(n, k)

            def main(c):
                n = c + 1
                for slot in range(STATES):
                    d, s = at_state(c, slot, SCAN)
                    if d.real:
                        scan(d, s)
                        if (s + 1) % H_RING == 0 and (d + 1).real:
                            keep_carry(d, s)
                    d, s = at_state(c, slot, BX)
                    if d.real and s in d.dve_b:
                        bx(d, s)
                    d, s = at_state(c, slot, TIMES_C)
                    if d.real and s in d.dve_c:
                        h_times_c(d, s)
                    if c.real:
                        front(c, slot + STATES)
                    if n.real:
                        front(n, slot)
                    if slot == FINISH_Y and (c + -1).real:
                        finish_y(c + -1)
                    for t in range(NT):
                        for m, at in ((c + -1, slot), (c + -2, slot + STATES)):
                            if at == slot_of(m + 2, f"O{t}") + 1 and m.real and not m.last:
                                add_residual(m, t)

            V.memset(bias_x3[PARTS * BC:SPREAD, :], 0.0).then_inc(s_nobias, 1)
            V.memset(ones[:], 1.0)
            V.memset(carry[:], 0.0).then_inc(s_carry, 1)
            whole_run(dve, main, steps, DVE_STEPS, first=2, last=CHUNKS - 3)
            for t in range(NT):
                add_residual(Chunk(CHUNKS - 1), t)

        @block.tensor
        def _(pe):
            mm = nc.tensor.matmul

            def bank_for(n, job):
                found = job_before(n, job)
                if found:
                    m, before = found
                    kind, j = before[0], int(before[1])
                    if kind == "T":
                        pe.wait_ge(s_xnT, m.count(1, 1))
                    elif kind == "R":
                        pe.wait_ge(s_logits, m.count(1, 1))
                    elif kind == "Z":
                        pe.wait_ge(s_xz, m.count(2 * KD, j + 1))
                    elif kind == "A":
                        pe.wait_ge(s_up, m.count(ET, j + 1))
                    elif kind == "O":
                        pe.wait_ge(s_out, m.count(NT, j + 1 - 2 * NT))
                    elif kind == "X":
                        pe.wait_ge(s_parts, m.count(1, 1))
                    elif kind == "D":
                        pe.wait_ge(s_dt, m.count(KD, j + 1))
                    elif kind == "M":
                        pe.wait_ge(s_hid, m.count(ET, j + 1))
                    elif kind == "G":
                        pe.wait_ge(s_gated, m.count(RT, j + 1))
                return job_ps[BANK[job]]

            def project_experts(c, t, ps):
                if t == 0:
                    pe.wait_ge(s_gated, c.count(RT, RT))
                    pe.wait_ge(s_hid, c.count(ET, ET))
                mm(ps, ones[:], bias_out[:], start=True, stop=False)
                for j in range(ET):
                    mm(ps, hid[:, c.parity, j, t * P:(t + 1) * P], w2[:, j], start=False, stop=False)

            def project_scan(c, t, ps):
                if t == 0:
                    pe.wait_ge(s_yz, c.count(1, 1))
                for k in range(KD):
                    ins = mm(ps, yz[:, k, t * P:(t + 1) * P], w_out[:, k], start=False, stop=(k == KD - 1))
                ins.then_inc(s_O, 1)

            def front_job(n, job):
                ps = bank_for(n, job)
                u = xz[:, n.parity]
                kind, j = job[0], int(job[1])
                if kind == "T" and n.first:
                    pe.wait_ge(s_ident, 16)
                if kind == "R" and n.first:
                    pe.wait_ge(s_first, 16 * N_FIRST)
                if kind == "A" and j == 0 and n.first:
                    pe.wait_ge(s_weights, 16 * N_WEIGHTS)
                if kind == "T":
                    pe.wait_ge(s_xn, n.count(1, 1))
                    for t in range(NT):
                        ins = nc.tensor.transpose(ps[:, t * P:(t + 1) * P], xn[:, t], ident[:])
                    ins.then_inc(s_T, 1)
                if kind == "R":
                    pe.wait_ge(s_xnT, n.count(1, 1))
                    for t in range(NT):
                        ins = mm(ps[:, t * EXPERTS:(t + 1) * EXPERTS], xn_t[:, t * P:(t + 1) * P], w_r[:],
                                 start=True, stop=True)
                    ins.then_inc(s_R, 1)
                if kind == "Z":
                    mm(ps[:], w_in[:, j * P:(j + 1) * P], xn_t[:], start=True, stop=True).then_inc(s_Z, 1)
                if kind == "A":
                    mm(ps[:], w1[:, EPT * j:EPT * (j + 1)], xn_t[:], start=True, stop=True).then_inc(s_A, 1)
                if kind == "O":
                    project_experts(n + -2, j, ps[:, 0:D])
                    project_scan(n + -2, j, ps[:, 0:D])
                if kind == "X":
                    pe.wait_ge(s_silu, n.count(2, 1))
                    pe.wait_ge(s_gates, n.count(1, 1))
                    for k in range(KD):
                        mm(ps[0:PARTS * BC, :], w_x3[:, k], u[:, k], start=(k == 0), stop=(k == KD - 1))
                    for t in range(NT):
                        ins = mm(ps[PARTS * BC:SPREAD, t * P:(t + 1) * P],
                                 gates3[:, t].rearrange("p q e -> p (q e)"), ident[:], start=True, stop=True)
                    ins.then_inc(s_X, 1)
                if kind == "D":
                    for k in range(KD):
                        ins = mm(ps[:], w_dt[:, k, j * P:(j + 1) * P], u[:, k], start=(k == 0), stop=(k == KD - 1))
                    ins.then_inc(s_D, 1)
                if kind == "M":
                    mm(ps[:], w3[:, EPT * j:EPT * (j + 1)], xn_t[:], start=True, stop=True).then_inc(s_M, 1)
                if kind == "G":
                    pe.wait_ge(s_parts, n.count(1, 1))
                    mm(ps[:], selector[:, STATES + j], parts[:, n.parity], start=True, stop=True).then_inc(s_Gps, 1)

            def spread_b(c, s):
                k = c.dve_b.index(s)
                if k == 0 and c.first:
                    pe.wait_ge(s_selector, 2)
                if k == 0:
                    pe.wait_ge(s_parts, c.count(1, 1))
                if k > 0 or c.since(1):
                    pe.wait_ge(s_bxd, c.count(len(DVE_B), k))
                mm(b_ps[:], selector[:, s], parts[:, c.parity], start=True, stop=True).then_inc(s_Bps, 1)

            def sum_states(c, s):
                if s + 1 in c.dve_c:
                    return
                if s in c.dve_c:
                    pe.wait_ge(s_hc_dve, 2 * c.dve_c.index(s) + 2)
                else:
                    pe.wait_ge(s_hc, c.count(STATES, c.pool_c_before(s) + 1))
                if s == 0 and c.since(1):
                    pe.wait_ge(s_yz, c.count(1, 0))
                for d in range(KD):
                    ins = mm(y_ps[:, d], ident[:], hc[:, s % Y_RING, d], start=(s == 0), stop=(s == STATES - 1))
                ins.then_inc(s_sum, 1)

            def jobs(n, slot):
                for job in JOBS:
                    if slot_of(n, job) == slot and job_lives(n, job):
                        front_job(n, job)

            def last_output(slot):
                c = Chunk(CHUNKS - 1)
                for t in range(NT):
                    if slot == EXPERTS_LAST[t]:
                        if t == 0:
                            pe.wait_ge(s_out, c.count(NT, 0))
                        if t == NT - 1:
                            pe.wait_ge(s_bxd, c.count(len(DVE_B), len(c.dve_b)))
                        project_experts(c, t, last_ps[t][:, 0:D])
                    if slot == STATES + FINISH_Y + 1:
                        project_scan(c, t, last_ps[t][:, 0:D])

            def main(c):
                for slot in range(STATES):
                    if c.k == CHUNKS:
                        last_output(slot + STATES)
                    d, s = at_state(c, slot, SUM)
                    if d.real and s > 0:
                        sum_states(d, s)
                    e, i = at_state(c, slot, SPREAD_B)
                    if e.real and i in e.dve_b and not e.last:
                        spread_b(e, i)
                    jobs(c, slot + STATES)
                    jobs(c + 1, slot)
                    if d.real and s == 0:
                        sum_states(d, s)
                    if c.last:
                        last_output(slot)
                    if e.real and i in e.dve_b and e.last:
                        spread_b(e, i)

            whole_run(pe, main, first=2, last=CHUNKS - 3)


_INS = ["L0_attn_x", "L0_attn_W_in", "L0_attn_b_in", "L0_attn_W_x", "L0_attn_b_x", "L0_attn_W_dt", "L0_attn_b_dt",
        "L0_attn_W_out", "L0_attn_b_out", "L0_attn_A_log", "L0_attn_D_param", "L0_ffn_router_w", "L0_ffn_router_b",
        "L0_ffn_routed_w1", "L0_ffn_routed_w3", "L0_ffn_routed_w2", "L0_ffn_shared_w1", "L0_ffn_shared_w3",
        "L0_ffn_shared_w2"]


def _constants(np):
    rows = np.zeros((SPREAD, STATES + EXPERTS), np.float32)
    mask = np.zeros((SPREAD, 2), np.float32)
    for q in range(PARTS):
        for s in range(STATES):
            rows[q * BC + s, s] = 1
        for e in range(EXPERTS):
            rows[PARTS * BC + q * EXPERTS + e, STATES + e] = 1
        for r in (slice(q * BC, (q + 1) * BC), slice(PARTS * BC + q * EXPERTS, PARTS * BC + (q + 1) * EXPERTS)):
            mask[r, 0] = -1.0 if q >= 1 else 0.0
            mask[r, 1] = -1.0 if q >= 2 else 0.0
    keep = np.zeros((P, 2, CHUNKS), np.float32)
    for c in range(CHUNKS):
        if c % CPB:
            keep[:, 0, c], keep[:, 1, c] = -BIG, BIG
    iota = np.tile(np.arange(EXPERTS, dtype=np.float32), (P, 1))
    return [("ident", np.eye(P, dtype=np.float32)), ("rows", rows), ("part_mask", mask), ("iota", iota),
            ("keep", keep)]


def kernel(**inputs):
    import numpy as _np
    import concourse.bacc as _bacc
    from concourse.bass_utils import run_bass_kernel_spmd as _run

    nc = _bacc.Bacc("TRN2", target_bir_lowering=False, num_devices=1)
    arrays, args = {}, []
    data = {n: _np.asarray(inputs[n]) for n in _INS}
    for n in ("L0_attn_b_in", "L0_attn_b_dt", "L0_attn_D_param"):
        data[n] = data[n].reshape(-1, P).T
    for name, a in list(data.items()) + _constants(_np):
        a = _np.ascontiguousarray(a)
        arrays[f"in_{name}_dram"] = a
        args.append(nc.dram_tensor(f"in_{name}_dram", a.shape, mybir.dt.from_np(a.dtype), kind="ExternalInput").ap())
    args.append(nc.dram_tensor("bc_rows", (2, BC, CHUNK), F32, kind="Internal").ap())
    args.append(nc.dram_tensor("out_dram", (BATCH, SEQ, D), F32, kind="ExternalOutput").ap())
    mixed_layer_program(nc, *args)
    r = _run(nc, [arrays], core_ids=[0])
    return r.results[0]["out_dram"]
```
